# Optimizing a Trainium2 kernel written in Bass

```python
import numpy as np
import jax
import jax.numpy as jnp

def _softmax(x, axis=-1):
    return jax.nn.softmax(x, axis=axis)

def _gelu(x):
    return jax.nn.gelu(x, approximate=True)

def _silu(x):
    return jax.nn.silu(x)

def _sigmoid(x):
    return jax.nn.sigmoid(x)

def _layernorm(x, axis=-1, eps=1e-05):
    m = jnp.mean(x, axis=axis, keepdims=True)
    v = jnp.var(x, axis=axis, keepdims=True)
    return (x - m) / jnp.sqrt(v + eps)

def _scatter_add(tgt, idx, src, axis=0):
    return tgt.at[idx].add(src)

def _segment_sum(src, seg, n):
    return jax.ops.segment_sum(src, seg, n)
kernel_name = 'mk_audio_tower_d1_tok_audfeat512_r4_f1a555'

def setup_inputs(seed: int=0):
    np.random.seed(seed)
    _w = jnp.asarray

    def _rec_inputs():
        import jax
        import jax.numpy as jnp
        _rk = jax.random.key(seed)
        x = -0.000124254 + 0.999853 * jax.random.normal(jax.random.fold_in(_rk, 1), (64, 375, 128), jnp.float32)
        return x
    x = _rec_inputs()

    def _L0_tok_setup():
        import jax, jax.numpy as jnp
        import numpy as np
        CONTEXT_LEN = 3
        SUBSAMPLING = 3
        key = jax.random.key(seed)
        k1, k2, k3 = jax.random.split(key, 3)
        mb, T, D = (64, 250, 128)
        out_dim = 128
        inp = jax.random.normal(k1, (mb, T, D), dtype=jnp.float32)
        weight = jax.random.normal(k2, (out_dim, D * CONTEXT_LEN), dtype=jnp.float32) * 0.02
        bias = jax.random.normal(k3, (out_dim,), dtype=jnp.float32) * 0.02
        return {'input': inp, 'weight': weight, 'bias': bias}
    _L0_tok_all = _L0_tok_setup()
    _L0_tok_in = {k: v for k, v in _L0_tok_all.items() if k in ('weight', 'bias')}
    del _L0_tok_all

    def _L0_attn_setup():
        import jax, jax.numpy as jnp
        import numpy as np
        B, T, C = (4, 1024, 128)

        def _rope_tables(T, C):
            pos = jnp.arange(T - 1, -1, -1, dtype=jnp.float32)
            dim = jnp.arange(C // 2, dtype=jnp.float32)
            angle = pos[:, None] * dim[None, :]
            return (jnp.cos(angle), jnp.sin(angle))

        def _rotate(z, cos, sin):
            Bz, Tz, Cz = z.shape
            zp = z.reshape(Bz, Tz, Cz // 2, 2)
            z0, z1 = (zp[..., 0], zp[..., 1])
            r0 = cos * z0 - sin * z1
            r1 = sin * z0 + cos * z1
            return jnp.stack([r0, r1], axis=-1).reshape(Bz, Tz, Cz)
        key = jax.random.key(seed)
        ks = jax.random.split(key, 9)
        s = 0.02
        inp = {'x': jax.random.normal(ks[0], (B, T, C), dtype=jnp.float32), 'Wk': jax.random.normal(ks[1], (C, C), dtype=jnp.float32) * s, 'bk': jax.random.normal(ks[2], (C,), dtype=jnp.float32) * s, 'Wq': jax.random.normal(ks[3], (C, C), dtype=jnp.float32) * s, 'bq': jax.random.normal(ks[4], (C,), dtype=jnp.float32) * s, 'Wv': jax.random.normal(ks[5], (C, C), dtype=jnp.float32) * s, 'bv': jax.random.normal(ks[6], (C,), dtype=jnp.float32) * s, 'Wp': jax.random.normal(ks[7], (C, C), dtype=jnp.float32) * s, 'bp': jax.random.normal(ks[8], (C,), dtype=jnp.float32) * s}
        return inp
    _L0_attn_all = _L0_attn_setup()
    _L0_attn_in = {k: v for k, v in _L0_attn_all.items() if k in ('Wk', 'bk', 'Wq', 'bq', 'Wv', 'bv', 'Wp', 'bp')}
    del _L0_attn_all

    def _L0_ffn_setup():
        import jax, jax.numpy as jnp
        import numpy as np
        B, S, D, F, E, NS, K = (2, 512, 128, 512, 8, 2, 2)
        key = jax.random.key(seed)
        ks = jax.random.split(key, 6)
        scale = 0.02

        def p(k, shape):
            return jax.random.normal(k, shape, jnp.float32) * scale
        return {'x': jax.random.normal(ks[0], (B, S, D), jnp.float32), 'gate_w': p(ks[1], (E, D)), 'gate_b': jnp.zeros((E,), jnp.float32), 'sw1': p(ks[2], (NS, F, D)), 'sb1': jnp.zeros((NS, F), jnp.float32), 'sw2': p(ks[3], (NS, D, F)), 'sb2': jnp.zeros((NS, D), jnp.float32), 'rw1': p(ks[4], (E, F, D)), 'rb1': jnp.zeros((E, F), jnp.float32), 'rw2': p(ks[5], (E, D, F)), 'rb2': jnp.zeros((E, D), jnp.float32)}
    _L0_ffn_all = _L0_ffn_setup()
    _L0_ffn_in = {k: v for k, v in _L0_ffn_all.items() if k in ('gate_w', 'gate_b', 'sw1', 'sb1', 'sw2', 'sb2', 'rw1', 'rb1', 'rw2', 'rb2')}
    del _L0_ffn_all
    return {'x': x, 'L0_tok_weight': _L0_tok_in['weight'], 'L0_tok_bias': _L0_tok_in['bias'], 'L0_attn_Wk': _L0_attn_in['Wk'], 'L0_attn_bk': _L0_attn_in['bk'], 'L0_attn_Wq': _L0_attn_in['Wq'], 'L0_attn_bq': _L0_attn_in['bq'], 'L0_attn_Wv': _L0_attn_in['Wv'], 'L0_attn_bv': _L0_attn_in['bv'], 'L0_attn_Wp': _L0_attn_in['Wp'], 'L0_attn_bp': _L0_attn_in['bp'], 'L0_ffn_gate_w': _L0_ffn_in['gate_w'], 'L0_ffn_gate_b': _L0_ffn_in['gate_b'], 'L0_ffn_sw1': _L0_ffn_in['sw1'], 'L0_ffn_sb1': _L0_ffn_in['sb1'], 'L0_ffn_sw2': _L0_ffn_in['sw2'], 'L0_ffn_sb2': _L0_ffn_in['sb2'], 'L0_ffn_rw1': _L0_ffn_in['rw1'], 'L0_ffn_rb1': _L0_ffn_in['rb1'], 'L0_ffn_rw2': _L0_ffn_in['rw2'], 'L0_ffn_rb2': _L0_ffn_in['rb2']}

def reference(x, L0_tok_weight, L0_tok_bias, L0_attn_Wk, L0_attn_bk, L0_attn_Wq, L0_attn_bq, L0_attn_Wv, L0_attn_bv, L0_attn_Wp, L0_attn_bp, L0_ffn_gate_w, L0_ffn_gate_b, L0_ffn_sw1, L0_ffn_sb1, L0_ffn_sw2, L0_ffn_sb2, L0_ffn_rw1, L0_ffn_rb1, L0_ffn_rw2, L0_ffn_rb2):
    import jax
    import jax.numpy as jnp

    def _L0_tok_ref(input, weight, bias):
        import jax, jax.numpy as jnp
        import numpy as np
        CONTEXT_LEN = 3
        SUBSAMPLING = 3
        mb, T, D = input.shape
        l = CONTEXT_LEN
        N = T - l + 1
        spliced = jnp.concatenate([input[:, i:i + N, :] for i in range(l)], axis=-1)
        if SUBSAMPLING > 1:
            spliced = spliced[:, ::SUBSAMPLING, :]
        return jnp.einsum('bnk,ok->bno', spliced, weight) + bias

    def _L0_attn_ref(x, Wk, bk, Wq, bq, Wv, bv, Wp, bp):
        import jax, jax.numpy as jnp
        import numpy as np
        B, T, C = (4, 1024, 128)

        def _rope_tables(T, C):
            pos = jnp.arange(T - 1, -1, -1, dtype=jnp.float32)
            dim = jnp.arange(C // 2, dtype=jnp.float32)
            angle = pos[:, None] * dim[None, :]
            return (jnp.cos(angle), jnp.sin(angle))

        def _rotate(z, cos, sin):
            Bz, Tz, Cz = z.shape
            zp = z.reshape(Bz, Tz, Cz // 2, 2)
            z0, z1 = (zp[..., 0], zp[..., 1])
            r0 = cos * z0 - sin * z1
            r1 = sin * z0 + cos * z1
            return jnp.stack([r0, r1], axis=-1).reshape(Bz, Tz, Cz)
        Bx, Tx, Cx = x.shape
        k = x @ Wk + bk
        q = x @ Wq + bq
        v = x @ Wv + bv
        cos, sin = _rope_tables(Tx, Cx)
        k = _rotate(k, cos, sin)
        q = _rotate(q, cos, sin)
        wei = jnp.einsum('btc,bsc->bts', k, q) * Cx ** (-0.5)
        mask = jnp.tril(jnp.ones((Tx, Tx), dtype=bool))
        wei = jnp.where(mask, wei, -jnp.inf)
        wei = jax.nn.softplus(wei)
        out = wei @ v
        out = out @ Wp + bp
        return out

    def _L0_ffn_ref(x, gate_w, gate_b, sw1, sb1, sw2, sb2, rw1, rb1, rw2, rb2):
        import jax, jax.numpy as jnp
        import numpy as np
        B, S, D, F, E, NS, K = (2, 512, 128, 512, 8, 2, 2)
        b, s, d = x.shape
        t = x.reshape(-1, d)
        T = t.shape[0]
        hs = jax.nn.gelu(jnp.einsum('td,nfd->ntf', t, sw1) + sb1[:, None, :], approximate=False)
        shared = jnp.einsum('ntf,ndf->td', hs, sw2) + sb2.sum(axis=0)
        logits = t @ gate_w.T + gate_b
        probs = jax.nn.softmax(logits, axis=-1)
        top_v, top_i = jax.lax.top_k(probs, K)
        cw = jnp.zeros_like(probs).at[jnp.arange(T)[:, None], top_i].add(top_v)
        hr = jax.nn.gelu(jnp.einsum('td,efd->etf', t, rw1) + rb1[:, None, :], approximate=False)
        oe = jnp.einsum('etf,edf->etd', hr, rw2) + rb2[:, None, :]
        routed = jnp.einsum('etd,te->td', oe, cw)
        return (shared + routed).reshape(b, s, d)
    h = _L0_tok_ref(x, L0_tok_weight, L0_tok_bias)
    h = h + _L0_attn_ref(_layernorm(h, axis=-1), L0_attn_Wk, L0_attn_bk, L0_attn_Wq, L0_attn_bq, L0_attn_Wv, L0_attn_bv, L0_attn_Wp, L0_attn_bp)
    h = h + _L0_ffn_ref(_layernorm(h, axis=-1), L0_ffn_gate_w, L0_ffn_gate_b, L0_ffn_sw1, L0_ffn_sb1, L0_ffn_sw2, L0_ffn_sb2, L0_ffn_rw1, L0_ffn_rb1, L0_ffn_rw2, L0_ffn_rb2)
    return h

_drawn_inputs = setup_inputs


def setup_inputs(seed=0):
    import zlib

    import numpy as np

    out = dict(_drawn_inputs(seed))
    spreads = {'L0_ffn_gate_b': (0.0, 0.1),
     'L0_ffn_sb1': (0.0, 0.1),
     'L0_ffn_sb2': (0.0, 0.1),
     'L0_ffn_rb1': (0.0, 0.8),
     'L0_ffn_rb2': (0.0, 0.1)}
    factors = {'L0_attn_Wk': 3.109,
     'L0_attn_bk': 8.0,
     'L0_attn_Wq': 3.102,
     'L0_attn_bq': 8.0,
     'L0_ffn_rw1': 2.691}
    for name, (base, spread) in spreads.items():
        noise = np.random.default_rng([zlib.crc32(name.encode()), seed]).standard_normal(out[name].shape)
        drawn = base * np.exp(spread * noise) if base else spread * noise
        out[name] = jnp.asarray(drawn.astype(out[name].dtype))
    for name, factor in factors.items():
        out[name] = (out[name] * factor).astype(out[name].dtype)
    return out
```

```python
from contextlib import ExitStack

import concourse.bass as bass
from concourse import mybir

F32 = mybir.dt.float32
F16 = mybir.dt.float16
BF16 = mybir.dt.bfloat16
I32 = mybir.dt.int32
ALU = mybir.AluOpType
ACT = mybir.ActivationFunctionType
X = mybir.AxisListType.X
ABSMAX = bass.bass_isa.ReduceOp.max

P = 128
B = 64
T = 125
CTX = 3
D = 128
E = 8
NS = 2
NE = E + NS
F = 512
FC = F // P
TOP = 2
EPS = 1e-5
GROUP = 4
NG = B // GROUP
GT = GROUP * T
TILE = 256
SUB = TILE // P
SLOTS_USED = B * T * TOP
NTILES = (SLOTS_USED + E * (TILE - 1)) // TILE
SLOTS = NTILES * TILE
MAXT = -(-B * T // TILE)
SJ = B // 2
SJA = 16
WCOLS = NE * F
WSTEP = WCOLS // NG
TOPBITS = 0x7F800000
ZROWS = 2
EXP_LN_TABLE = 6
GELU_TABLE = 10
LIFT = 2.0 ** 14
LEAST = 2.0 ** -40


def build(nc, d, out):
    x_tok = nc.dram_tensor("x_tok", [B * T, 2 * D], F16).ap()
    x_slots = nc.dram_tensor("x_slots", [SLOTS, 2 * D], F16).ap()
    y_slots = nc.dram_tensor("y_slots", [SLOTS, D], F32).ap()

    with ExitStack() as ctx:
        def sb(name, shape, dt):
            return ctx.enter_context(nc.sbuf_tensor(name, shape, dt))

        def psum(name, shape, dt):
            return ctx.enter_context(nc.psum_tensor(name, shape, dt))

        def sem(name):
            return ctx.enter_context(nc.semaphore(name))

        pre_ps = psum("pre_ps", [P, 2, 2, 512], F32)
        xp_ps = psum("xp_ps", [P, 2, 512], F32)
        y_ps = psum("y_ps", [P, 2, 512], F32)
        q_ps, qs_ps = pre_ps[:, 0, 0, :], pre_ps[:, 0, 1, :]
        k_ps, ks_ps = pre_ps[:, 1, 0, :], pre_ps[:, 1, 1, :]
        v_ps, wp_ps = q_ps, qs_ps
        s_ps, t1_ps = xp_ps[:, 0, :], xp_ps[:, 1, :]
        lg_ps = t1_ps
        t2_ps, h_ps = y_ps[:, 0, :], y_ps[:, 1, :]
        pv_ps = t2_ps

        wt = sb("wt", [P, CTX, D], F32)
        wmat = sb("wmat", [P, 6, D], F32)
        rope = sb("rope", [P, 4, T], F32)
        colb = sb("colb", [P, 4], F32)
        rowb = sb("rowb", [P, 5, D], F32)
        gateb = sb("gateb", [P, E], F32)
        ident = sb("ident", [P, P], F32)
        identh = sb("identh", [P, P], F16)
        maskl = sb("maskl", [P, 2, P], BF16)
        tri = sb("tri", [P, 2, P], BF16)
        counts_const = sb("counts_const", [P, MAXT + NTILES + 2 * E], F32)
        tile_steps = counts_const[:, 0:MAXT]
        tile_ids = counts_const[:, MAXT:MAXT + NTILES]
        prefer_low = counts_const[:, MAXT + NTILES:MAXT + NTILES + E]
        gatew = sb("gatew", [P, E], F32)
        b1 = sb("b1", [P, NE * FC], F32)
        b2 = sb("b2", [P, E, D], F32)
        epsc = sb("epsc", [P, 2, GROUP], F32)
        ones64 = sb("ones64", [P, B], F32)
        zeros = sb("zeros", [P, ZROWS * 2 * D], F16)
        w32 = sb("w32", [P, 2, WCOLS], F32)
        whi = sb("whi", [P, 2, WCOLS], F16)
        wlo = sb("wlo", [P, 2, WCOLS], F16)
        gsplit = sb("gsplit", [P, 2, E], F16)
        mx = sb("mx", [P, 4], F32)
        mxall = sb("mxall", [P, 4], F32)
        pw = sb("pw", [P, 4], F32)
        up = sb("up", [P, 4], F32)
        down = sb("down", [P, 4], F32)
        yscale = sb("yscale", [P, 1], F32)

        x_in = sb("x_in", [P, CTX, GT], F32)
        h_all = sb("h_all", [P, B, D], F32)
        st1 = sb("st1", [P, GROUP, 6], F32)
        mv1 = sb("mv1", [P, GROUP, 2], F32)
        rs1 = sb("rs1", [P, GROUP], F32)
        ve1 = sb("ve1", [P, GROUP], F32)
        ln = sb("ln", [P, GROUP, D], F32)
        ln_t = sb("ln_t", [P, GT], F32)
        rparts = sb("rparts", [P, 4, GT], F32)
        q_t = sb("q_t", [P, GT], F32)
        k_t = sb("k_t", [P, GT], F32)
        v_tok = sb("v_tok", [P, GROUP, D], F32)
        sp = sb("sp", [P, GT], F32)
        wei = sb("wei", [P, GT], F32)
        att_t = sb("att_t", [P, GT], F32)
        st2 = sb("st2", [P, GROUP, 6], F32)
        mv2 = sb("mv2", [P, GROUP, 2], F32)
        rs2 = sb("rs2", [P, GROUP], F32)
        ve2 = sb("ve2", [P, GROUP], F32)
        xn = sb("xn", [P, GROUP, D], F32)
        xsplit = sb("xsplit", [P, GROUP, 2, D], F16)
        xt_all = sb("xt_all", [P, 2, B * T], F16)
        logits = sb("logits", [P, B, E], F32)

        chosen = sb("chosen", [P, B * E], BF16)
        rvec = sb("rvec", [P, 4, B], F32)
        gatev = sb("gatev", [P, TOP, B], F32)
        te = sb("te", [P, 4, E], F32)
        posf = sb("posf", [P, B, TOP], F32)
        pos = sb("pos", [P, B, TOP], I32)
        tile_exf = sb("tile_exf", [1, NTILES], F32)
        tile_ex = sb("tile_ex", [1, NTILES], I32)

        w32f = w32[:, :, :].rearrange("p a n -> p (a n)")
        gel = w32f[:, 0:2 * FC * TILE].rearrange("p (b n) -> p b n", b=2)
        o = 2 * FC * TILE
        gat = w32f[:, o:o + 2 * GROUP * TOP * D].rearrange("p (b g k n) -> p b g k n", b=2, g=GROUP, k=TOP)
        o += 2 * GROUP * TOP * D
        y_out = w32f[:, o:o + 2 * SUB * D].rearrange("p (b s n) -> p b s n", b=2, s=SUB)
        o += 2 * SUB * D
        cmp = w32f[:, o:o + 1024]
        o += 1024
        ra, rc = (w32f[:, o + n * B * E:o + (n + 1) * B * E].rearrange("p (b e) -> p b e", e=E) for n in range(2))
        o += 2 * B * E
        oh = w32f[:, o:o + TOP * B * E].rearrange("p (k b e) -> p k b e", k=TOP, e=E)
        o += TOP * B * E
        run = w32f[:, o:o + B * E].rearrange("p (e b) -> p e b", e=E)
        o += B * E
        hhi, hlo = (w32f[:, o + n * FC * TILE:o + (n + 1) * FC * TILE].bitcast(F16)
                    .rearrange("p (b f n) -> p b f n", b=2, f=FC) for n in range(2))
        o += 2 * FC * TILE
        assert o <= 2 * WCOLS
        xr_t = sb("xr_t", [P, 2, 2, TILE], F16)
        rpf = rparts[:].rearrange("p a n -> p (a n)")
        xs = rpf[:, 0:2 * GROUP * D].bitcast(F16).rearrange("p (b g n) -> p b g n", b=2, g=GROUP)
        o = 2 * GROUP * D
        xr_in = rpf[:, o:o + 2 * SUB * D].bitcast(F16).rearrange("p (b s n) -> p b s n", b=2, s=SUB)
        idx = sb("idx", [P, 2, GROUP, TOP], I32)

        s_setup = sem("setup_loaded")
        s_w32 = sem("weights_loaded")
        s_const = sem("consts_set")
        s_zero = sem("slots_zeroed")
        s_mx = sem("maxima_taken")
        s_mxall = sem("maxima_joined")
        s_scale = sem("scales_chain")
        s_gs = sem("gate_split")
        s_x = sem("x_loaded")
        s_h_mm = sem("h_products")
        s_h = sem("h_stored")
        s_st1a, s_st1, s_ve1, s_rs1, s_ln = (sem(n) for n in ("ln1_stats", "ln1_moments", "ln1_var_eps", "ln1_rstd", "ln1_done"))
        s_t1, s_lnt = sem("ln1_transposed"), sem("ln1_t_stored")
        s_qk, s_rp, s_rope = sem("qk_products"), sem("rope_parts"), sem("rope_done")
        s_v_mm, s_v = sem("v_products"), sem("v_stored")
        s_s, s_abs, s_exp, s_lnp, s_wei = (sem(n) for n in ("scores", "score_abs", "score_exp", "score_log", "weights_done"))
        s_pv, s_att, s_wp, s_hb, s_h2 = (sem(n) for n in ("pv_products", "att_stored", "wp_products", "h_plus_bp", "h2_done"))
        s_st2a, s_st2, s_ve2, s_rs2, s_xn = (sem(n) for n in ("ln2_stats", "ln2_moments", "ln2_var_eps", "ln2_rstd", "ln2_done"))
        s_xhi, s_xlo, s_xtok, s_hb2 = (sem(n) for n in ("x_high", "x_low", "x_tok_stored", "h2_plus_b2"))
        s_t2, s_xt, s_lg_mm, s_lg = (sem(n) for n in ("x_transposed", "x_t_stored", "gate_products", "logits_stored"))
        s_whi, s_wlo = sem("w_high"), sem("w_low")
        s_r = sem("routing_chain")
        s_rexp, s_rank = sem("router_exp"), sem("rank_products")
        s_routed = sem("routing_done")
        s_chosen = sem("experts_chosen")
        s_xs = [sem(f"x_staged{p}") for p in range(2)]
        s_idx = sem("indices_staged")
        s_scat = [sem(f"scattered{p}") for p in range(2)]
        s_xr = [sem(f"tile_loaded{p}") for p in range(2)]
        s_xp = [sem(f"tile_transposed{p}") for p in range(2)]
        s_xrt = [sem(f"tile_t_stored{p}") for p in range(2)]
        s_pre = [sem(f"pre_half{p}") for p in range(2)]
        s_gelu, s_hhi, s_hlo = sem("gelu_done"), sem("hidden_high"), sem("hidden_low")
        s_y_mm, s_ysh = sem("unit_outputs"), sem("shared_added")
        s_yr = [sem(f"tile_output{p}") for p in range(2)]
        s_yst = [sem(f"tile_stored{p}") for p in range(2)]
        s_gat = [sem(f"gathered{p}") for p in range(2)]
        s_half, s_out = sem("first_expert_added"), sem("out_stored")
        s_comb = [sem(f"experts_added{p}") for p in range(2)]

        block = ctx.enter_context(nc.Block())

        def done(eng, s, n, step=1):
            if isinstance(n, int):
                if n > 0:
                    eng.wait_ge(s, n * step)
            else:
                eng.wait_ge(s, n * step if step != 1 else n)

        def done_apart(eng, s, n, step=1):
            if isinstance(n, int):
                done(eng, s, n, step)
            else:
                value = eng.to_reg(n * step if step != 1 else n)
                eng.wait_ge(s_const, 1)
                eng.wait_ge(s, value)

        def upto(n):
            return min(n, NG) if isinstance(n, int) else n

        def pipeline(eng, stages):
            first = min(-lag for _, lag in stages)
            last = max(NG - 1 - lag for _, lag in stages)
            lo = max(-lag for _, lag in stages) + 1
            hi = min(NG - lag for _, lag in stages)

            def step(i):
                for stage, lag in stages:
                    if not isinstance(i, int) or 0 <= i + lag < NG:
                        stage(i + lag)

            for i in range(first, lo):
                step(i)
            with eng.Fori(lo, hi) as i:
                step(i)
            for i in range(hi, last + 1):
                step(i)

        N_SETUP = 15

        @block.sync
        def _(sp_eng):
            eng = sp_eng
            loads = [(wt[:], d["wt"]), (rowb[:], d["rowb"]), (ident[:], d["ident"]), (wmat[:], d["wmat"]),
                     (rope[:], d["rope"]), (colb[:], d["colb"]), (maskl[:], d["maskl"]), (identh[:], d["identh"]),
                     (gateb[:], d["gateb"]), (gatew[:], d["gatew"]), (tri[:], d["tri"]),
                     (counts_const[:], d["counts"]), (b1[:, 0:E * FC], d["rb1"]), (b1[:, E * FC:], d["sb1"]),
                     (b2[:], d["rb2"])]
            assert len(loads) == N_SETUP
            x_d = d["x"]

            def load_x(g):
                done(eng, s_h_mm, g)
                eng.dma_start(x_in[:], x_d[:, :, bass.ds(g * GT, GT)]).then_inc(s_x, 16)

            def store_x_tok(g):
                done_apart(eng, s_xlo, g + 1)
                eng.dma_start(x_tok[bass.ds(g * GT, GT), :].rearrange("(b t) n -> t b n", t=T),
                              xsplit[0:T].rearrange("p b h n -> p b (h n)")).then_inc(s_xtok, 16)

            for n, (dst, src) in enumerate(loads):
                eng.dma_start(dst, src).then_inc(s_setup, 16)
                if n == 1:
                    load_x(0)
            eng.dma_start(w32[:, 0, 0:E * F], d["rw1"]).then_inc(s_w32, 16)
            eng.dma_start(w32[:, 0, E * F:], d["sw1"]).then_inc(s_w32, 16)
            eng.dma_start(w32[:, 1, 0:E * F], d["rw2"]).then_inc(s_w32, 16)
            eng.dma_start(w32[:, 1, E * F:], d["sw2"]).then_inc(s_w32, 16)
            eng.wait_ge(s_const, 3)
            rows = SLOTS // P // ZROWS
            eng.dma_start(x_slots.rearrange("(p a r) n -> p a (r n)", p=P, a=rows),
                          zeros[:].rearrange("p (a n) -> p a n", a=1).to_broadcast([P, rows, ZROWS * 2 * D])
                          ).then_inc(s_zero, 16)
            for g in range(1, 3):
                load_x(g)
            with eng.Fori(3, NG) as g:
                load_x(g)
                store_x_tok(g - 3)
            for g in range(NG - 3, NG):
                store_x_tok(g)

            eng.wait_ge(s_xtok, 16 * NG)

            def stage_x(n, par):
                done_apart(eng, s_scat[par], n, 16 * GROUP * TOP)
                eng.dma_start(xs[0:T, par], x_tok[bass.ds((n * 2 + par) * GT, GT), :]
                              .rearrange("(b t) n -> t b n", t=T)).then_inc(s_xs[par], 16)
            for par in range(2):
                stage_x(0, par)
            with eng.Fori(1, NG // 2) as n:
                for par in range(2):
                    stage_x(n, par)

            for par in range(2):
                eng.wait_ge(s_scat[par], 16 * GROUP * TOP * NG // 2)

            def load_tile(n, par):
                done_apart(eng, s_xp[par], n)
                eng.dma_start(xr_in[:, par], x_slots[bass.ds((n * 2 + par) * TILE, TILE), :]
                              .rearrange("(s p) n -> p s n", p=P)).then_inc(s_xr[par], 16)

            def store_tile(n, par):
                done_apart(eng, s_yr[par], n + 1)
                eng.dma_start(y_slots[bass.ds((n * 2 + par) * TILE, TILE), :]
                              .rearrange("(s p) n -> p s n", p=P), y_out[:, par]).then_inc(s_yst[par], 16)
            for n in range(2):
                for par in range(2):
                    load_tile(n, par)
            with eng.Fori(2, NTILES // 2) as n:
                for par in range(2):
                    load_tile(n, par)
                    store_tile(n - 2, par)
            for n in (NTILES // 2 - 2, NTILES // 2 - 1):
                for par in range(2):
                    store_tile(n, par)

            with eng.Fori(0, NG // 2) as n:
                for par in range(2):
                    g = n * 2 + par
                    done_apart(eng, s_comb[par], n + 1)
                    eng.dma_start(out[bass.ds(g * GROUP, GROUP)].rearrange("b t n -> t b n"),
                                  h_all[0:T, bass.ds(g * GROUP, GROUP), :]).then_inc(s_out, 16)
            eng.wait_ge(s_out, 16 * NG)
            eng.wait_ge(s_zero, 16)

        @block.gpsimd
        def _(pool):
            eng = pool
            nc.gpsimd.memset(epsc[:, 0], EPS)
            nc.gpsimd.memset(epsc[:, 1], -0.5)
            nc.gpsimd.memset(ones64[:], 1.0).then_inc(s_const, 1)
            nc.gpsimd.memset(zeros[:], 0.0).then_inc(s_const, 2)
            eng.wait_ge(s_const, 3)
            eng.wait_ge(s_mx, 4)
            nc.gpsimd.partition_all_reduce(mxall[:], mx[:], P, ABSMAX).then_inc(s_mxall, 1)

            def rstd1(g):
                done(eng, s_st1, g + 1)
                nc.gpsimd.tensor_tensor(ve1[0:T], mv1[0:T, :, 1], epsc[0:T, 0], ALU.add).then_inc(s_ve1, 1)
                done(eng, s_ve1, g + 1)
                nc.gpsimd.tensor_tensor(rs1[0:T], ve1[0:T], epsc[0:T, 1], ALU.pow).then_inc(s_rs1, 1)

            def add_bp(g):
                done(eng, s_ln, g + 1)
                hg = h_all[0:T, bass.ds(g * GROUP, GROUP), :]
                nc.gpsimd.tensor_tensor(hg, hg, rowb[0:T, 2:3, :].to_broadcast([T, GROUP, D]), ALU.add).then_inc(s_hb, 1)

            def rope_add(g):
                done(eng, s_s, g)
                done(eng, s_rp, g + 1)
                nc.gpsimd.tensor_tensor(q_t[:], rparts[:, 0], rparts[:, 1], ALU.add)
                nc.gpsimd.tensor_tensor(k_t[:], rparts[:, 2], rparts[:, 3], ALU.add).then_inc(s_rope, 1)

            def rstd2(g):
                done(eng, s_st2, g + 1)
                nc.gpsimd.tensor_tensor(ve2[0:T], mv2[0:T, :, 1], epsc[0:T, 0], ALU.add).then_inc(s_ve2, 1)
                done(eng, s_ve2, g + 1)
                nc.gpsimd.tensor_tensor(rs2[0:T], ve2[0:T], epsc[0:T, 1], ALU.pow).then_inc(s_rs2, 1)

            def add_b2(g):
                done(eng, s_xn, g + 1)
                hg = h_all[0:T, bass.ds(g * GROUP, GROUP), :]
                nc.gpsimd.tensor_tensor(hg, hg, rowb[0:T, 3:4, :].to_broadcast([T, GROUP, D]), ALU.add).then_inc(s_hb2, 1)

            pipeline(eng, [(rstd2, -1), (add_b2, -1), (rope_add, 1), (rstd1, 2), (add_bp, 2)])

            def stage_idx(n, par, passes):
                nc.gpsimd.tensor_copy(idx[0:T, par], pos[0:T, bass.ds((n * 2 + par) * GROUP, GROUP), :]).then_inc(s_idx, 1)
                done_apart(eng, s_idx, n * 2 + par + 1 + passes * NG)

            def scatter(n, par):
                done_apart(eng, s_scat[par], n, 16 * GROUP * TOP)
                stage_idx(n, par, 0)
                done_apart(eng, s_xs[par], n + 1, 16)
                for b in range(GROUP):
                    for k in range(TOP):
                        nc.gpsimd.indirect_dma_start(
                            x_slots, bass.IndirectOffsetOnAxis(ap=idx[0:T, par, b, k:k + 1], axis=0),
                            xs[0:T, par, b, :], None).then_inc(s_scat[par], 16)

            def gather(n, par):
                done_apart(eng, s_gat[par], n, 16 * GROUP * TOP)
                done_apart(eng, s_comb[par], n)
                stage_idx(n, par, 1)
                for b in range(GROUP):
                    for k in range(TOP):
                        nc.gpsimd.indirect_dma_start(
                            gat[0:T, par, b, k, :], None,
                            y_slots, bass.IndirectOffsetOnAxis(ap=idx[0:T, par, b, k:k + 1], axis=0),
                        ).then_inc(s_gat[par], 16)

            eng.wait_ge(s_routed, 1)
            eng.wait_ge(s_zero, 16)
            for par in range(2):
                scatter(0, par)
            with eng.Fori(1, NG // 2) as n:
                for par in range(2):
                    scatter(n, par)

            for par in range(2):
                eng.wait_ge(s_scat[par], 16 * GROUP * TOP * NG // 2)
                eng.wait_ge(s_yst[par], 16 * NTILES // 2)
            for par in range(2):
                gather(0, par)
            with eng.Fori(1, NG // 2) as n:
                for par in range(2):
                    gather(n, par)

        @block.tensor
        def _(pe):
            eng = pe

            def h_mm(g):
                done(eng, s_h, g)
                done(eng, s_x, g + 1, 16)
                for b in range(GROUP):
                    for c in range(CTX):
                        last = nc.tensor.matmul(h_ps[0:T, b * D:(b + 1) * D], x_in[:, c, b * T:(b + 1) * T], wt[:, c, :],
                                                start=(c == 0), stop=(c == CTX - 1))
                last.then_inc(s_h_mm, 1)

            def t1(g):
                done(eng, s_lg, g - 2)
                done(eng, s_lnt, g)
                done(eng, s_ln, g + 1)
                for b in range(GROUP):
                    last = nc.tensor.transpose(t1_ps[:, b * T:(b + 1) * T], ln[0:T, b, :], ident[0:T, 0:T])
                last.then_inc(s_t1, 1)

            def qk(g):
                done(eng, s_v, g)
                done(eng, s_h2, g - 1)
                done(eng, s_rp, g)
                done(eng, s_lnt, g + 1)
                for n, dst in enumerate((q_ps, qs_ps, k_ps, ks_ps)):
                    last = nc.tensor.matmul(dst[:, 0:GT], wmat[:, n, :], ln_t[:], start=True, stop=True)
                last.then_inc(s_qk, 1)

            def v_mm(g):
                done(eng, s_rp, g + 1)
                for b in range(GROUP):
                    last = nc.tensor.matmul(v_ps[0:T, b * D:(b + 1) * D], ln_t[:, b * T:(b + 1) * T], wmat[:, 4, :],
                                            start=True, stop=True)
                last.then_inc(s_v_mm, 1)

            def s_mm(g):
                done(eng, s_wei, g)
                done(eng, s_rope, g + 1)
                nc.tensor.matmul(s_ps[0:T, 0:GT], maskl[0:T, 0, 0:T],
                                 maskl[0:T, 1:2, 0:T].to_broadcast([T, GROUP, T]), start=True, stop=False)
                for b in range(GROUP):
                    c = slice(b * T, (b + 1) * T)
                    last = nc.tensor.matmul(s_ps[0:T, c], q_t[:, c], k_t[:, c], start=False, stop=(b == GROUP - 1))
                last.then_inc(s_s, 1)

            def pv(g):
                done(eng, s_xt, g)
                done(eng, s_v, g + 1)
                done(eng, s_wei, g + 1)
                for b in range(GROUP):
                    c = slice(b * T, (b + 1) * T)
                    last = nc.tensor.matmul(pv_ps[:, c], v_tok[0:T, b, :], wei[0:T, c], start=True, stop=True)
                last.then_inc(s_pv, 1)

            def wp(g):
                done(eng, s_rp, upto(g + 2))
                done(eng, s_att, g + 1)
                for b in range(GROUP):
                    last = nc.tensor.matmul(wp_ps[0:T, b * D:(b + 1) * D], att_t[:, b * T:(b + 1) * T], wmat[:, 5, :],
                                            start=True, stop=True)
                last.then_inc(s_wp, 1)

            t2_h = t2_ps.bitcast(F16)

            def t2(g):
                done(eng, s_att, g + 1)
                done(eng, s_xlo, g + 1)
                for h in range(2):
                    for b in range(GROUP):
                        c = h * 512 + b * P
                        last = nc.tensor.transpose(t2_h[:, c:c + T], xsplit[0:T, b, h, :], identh[0:T, 0:T])
                last.then_inc(s_t2, 1)

            def lg(g):
                done(eng, s_lnt, upto(g + 3))
                done(eng, s_gs, 2)
                done(eng, s_xt, g + 1)
                for b in range(GROUP):
                    xh = xt_all[:, 0, bass.ds(g * GT + b * T, T)]
                    xl = xt_all[:, 1, bass.ds(g * GT + b * T, T)]
                    dst = lg_ps[0:T, b * E:(b + 1) * E]
                    nc.tensor.matmul(dst, xh, gsplit[:, 0], start=True, stop=False)
                    nc.tensor.matmul(dst, xh, gsplit[:, 1], start=False, stop=False)
                    last = nc.tensor.matmul(dst, xl, gsplit[:, 0], start=False, stop=True)
                last.then_inc(s_lg_mm, 1)

            eng.wait_ge(s_setup, 16 * N_SETUP)
            pipeline(eng, [(s_mm, 0), (t1, 1), (qk, 1), (t2, -1), (h_mm, 2), (lg, -1), (pv, 0), (v_mm, 1), (wp, 0)])

            eng.wait_ge(s_chosen, 1)
            eng.wait_ge(s_h, NG)
            nc.tensor.matmul(y_ps[0:T, 0, :], tri[0:T, 0, 0:T], chosen[0:T], start=True, stop=True)
            nc.tensor.matmul(y_ps[0:T, 1, :], tri[0:T, 1, 0:T], chosen[0:T], start=True, stop=True).then_inc(s_rank, 1)

            def unit_up(u, par, x_hi, x_lo, n, col):
                done(eng, s_gelu, u - 1)
                for f in range(FC):
                    dst = pre_ps[:, par, f // 2, (f % 2) * TILE:(f % 2) * TILE + n]
                    hi = whi[:, 0, bass.ds(col + f * P, P)]
                    lo = wlo[:, 0, bass.ds(col + f * P, P)]
                    nc.tensor.matmul(dst, hi, x_hi, start=True, stop=False)
                    nc.tensor.matmul(dst, hi, x_lo, start=False, stop=False)
                    last = nc.tensor.matmul(dst, lo, x_hi, start=False, stop=True)
                    if f % 2:
                        last.then_inc(s_pre[f // 2], 1)

            def unit_down(u, par, m, dsts, col, first, final):
                done(eng, s_hlo, u + 1)
                for t in range(2):
                    for f in range(FC):
                        h = hhi[:, par, f, t * m:(t + 1) * m]
                        l = hlo[:, par, f, t * m:(t + 1) * m]
                        hi = whi[:, 1, bass.ds(col + f * P, P)]
                        lo = wlo[:, 1, bass.ds(col + f * P, P)]
                        nc.tensor.matmul(dsts[t], h, hi, start=first and f == 0, stop=False)
                        nc.tensor.matmul(dsts[t], h, lo, start=False, stop=False)
                        last = nc.tensor.matmul(dsts[t], l, hi, start=False, stop=final and f == FC - 1)
                last.then_inc(s_y_mm, 1)

            shared_dst = [y_ps[0:T, t, 0:D] for t in range(2)]

            def shared_up(j, s, base):
                cols = bass.ds(j * 2 * T, 2 * T)
                unit_up(j * 2 + s + base, s, xt_all[:, 0, cols], xt_all[:, 1, cols], 2 * T, (E + s) * F)

            def shared_down(j, s, base, routed_before):
                if s == 0:
                    done(eng, s_ysh, j)
                    if routed_before:
                        for p in range(2):
                            eng.wait_ge(s_yr[p], NTILES // 2)
                unit_down(j * 2 + s + base, s, T, shared_dst, (E + s) * F, s == 0, s == 1)

            xp_h = [xp_ps[:, p, :].bitcast(F16) for p in range(2)]

            def routed_transpose(n, par):
                done(eng, s_xrt[par], n)
                done(eng, s_xr[par], n + 1, 16)
                for h in range(2):
                    for s in range(SUB):
                        c = h * TILE + s * P
                        last = nc.tensor.transpose(xp_h[par][:, c:c + P], xr_in[:, par, s, h * D:(h + 1) * D], identh[:])
                last.then_inc(s_xp[par], 1)

            def expert_cols(n, par):
                return pe.value_load(tile_ex[0:1, bass.ds(n * 2 + par, 1)], min_val=0, max_val=E - 1) * F

            def routed_up(n, par, col):
                t = n * 2 + par
                done(eng, s_xrt[par], n + 1)
                unit_up(t + 2 * SJA, par, xr_t[:, par, 0], xr_t[:, par, 1], TILE, col)

            def routed_down(n, par, col):
                t = n * 2 + par
                done(eng, s_yr[par], n)
                unit_down(t + 2 * SJA, par, P, [y_ps[:, par, s * D:(s + 1) * D] for s in range(SUB)], col, True, True)

            eng.wait_ge(s_wlo, NG)
            eng.wait_ge(s_xt, NG)
            eng.wait_ge(s_routed, 1)
            shared_up(0, 0, 0)
            shared_up(0, 1, 0)
            for s in range(2):
                shared_down(0, s, 0, False)
                shared_up(1, s, 0)
            with eng.Fori(1, SJA - 1) as j:
                for s in range(2):
                    shared_down(j, s, 0, False)
                    shared_up(j + 1, s, 0)
            for par in range(2):
                routed_transpose(0, par)
                shared_down(SJA - 1, par, 0, False)
                routed_up(0, par, expert_cols(0, par))
            eng.wait_ge(s_ysh, SJA)

            def routed_step(n):
                for par in range(2):
                    routed_transpose(n + 1, par)
                    routed_down(n, par, expert_cols(n, par))
                    routed_up(n + 1, par, expert_cols(n + 1, par))
            routed_step(0)
            with eng.Fori(1, NTILES // 2 - 1) as n:
                routed_step(n)
            for par in range(2):
                routed_down(NTILES // 2 - 1, par, expert_cols(NTILES // 2 - 1, par))
                shared_up(SJA, par, NTILES)
            for s in range(2):
                shared_down(SJA, s, NTILES, True)
                shared_up(SJA + 1, s, NTILES)
            with eng.Fori(SJA + 1, SJ - 1) as j:
                for s in range(2):
                    shared_down(j, s, NTILES, False)
                    shared_up(j + 1, s, NTILES)
            for s in range(2):
                shared_down(SJ - 1, s, NTILES, False)

        @block.scalar
        def _(act):
            eng = act

            def load_table(table):
                eng.add_instruction(mybir.InstLoadActFuncSet(
                    name=nc.get_next_instruction_name(), engine=mybir.EngineType.Activation, act_func_set_id=table))

            def softplus_abs(g):
                done(eng, s_s, g + 1)
                nc.scalar.activation(sp[0:T], s_ps[0:T, 0:GT], ACT.Abs).then_inc(s_abs, 1)

            def softplus_log(g):
                done(eng, s_abs, g + 1)
                nc.scalar.activation(sp[0:T], sp[0:T], ACT.Exp, scale=-1.0).then_inc(s_exp, 1)
                done(eng, s_exp, g + 1)
                nc.scalar.activation(sp[0:T], sp[0:T], ACT.Ln, bias=1.0).then_inc(s_lnp, 1)

            def ln_t_out(g):
                done(eng, s_v_mm, g)
                done(eng, s_t1, g + 1)
                nc.scalar.activation(ln_t[:], t1_ps[:, 0:GT], ACT.Copy).then_inc(s_lnt, 1)

            def att_out(g):
                done(eng, s_wp, g)
                done(eng, s_pv, g + 1)
                nc.scalar.activation(att_t[:], pv_ps[:, 0:GT], ACT.Copy).then_inc(s_att, 1)

            def x_t_out(g):
                done_apart(eng, s_t2, g + 1)
                nc.scalar.activation(
                    xt_all[:, :, bass.ds(g * GT, GT)].rearrange("p h (b t) -> p h b t", b=GROUP),
                    t2_ps.bitcast(F16).rearrange("p (h b t) -> p h b t", h=2, b=GROUP)[:, :, :, 0:T], ACT.Copy).then_inc(s_xt, 1)

            def logits_out(g):
                done_apart(eng, s_lg_mm, g + 1)
                nc.scalar.activation(logits[0:T, bass.ds(g * GROUP, GROUP), :],
                                     lg_ps[0:T, 0:GROUP * E].rearrange("p (b e) -> p b e", e=E), ACT.Copy,
                                     scale=down[0:T, 3:4]).then_inc(s_lg, 1)

            def w_high(g):
                if isinstance(g, int) and g == 0:
                    eng.wait_ge(s_gs, 2)
                for n, scale in ((0, up[:, 0:1]), (1, up[:, 2:3])):
                    c = bass.ds(g * WSTEP, WSTEP)
                    last = nc.scalar.activation(whi[:, n, c], w32[:, n, c], ACT.Copy, scale=scale)
                last.then_inc(s_whi, 1)

            load_table(EXP_LN_TABLE)
            pipeline(eng, [(softplus_abs, 0), (ln_t_out, 1), (softplus_log, 0), (w_high, 0), (x_t_out, -1), (logits_out, -1), (att_out, 0)])

            eng.wait_ge(s_r, 3)
            nc.scalar.activation(ra[0:T], logits[0:T], ACT.Exp).then_inc(s_rexp, 1)

            def gelu(u, par, n, col):
                done_apart(eng, s_hlo, u - 1)
                for f in range(FC):
                    if f % 2 == 0:
                        done_apart(eng, s_pre[f // 2], u + 1)
                    last = nc.scalar.activation(gel[:, par, f * TILE:f * TILE + n],
                                                pre_ps[:, par, f // 2, (f % 2) * TILE:(f % 2) * TILE + n], ACT.Gelu,
                                                bias=b1[:, bass.ds(col + f, 1)], scale=down[:, 0:1])
                last.then_inc(s_gelu, 1)

            def xr_out(n, par):
                t = n * 2 + par
                done(eng, s_pre[1], t - 1 + 2 * SJA)
                done(eng, s_xp[par], n + 1)
                nc.scalar.activation(xr_t[:, par].rearrange("p h n -> p (h n)"),
                                     xp_ps[:, par, :].bitcast(F16)[:, 0:2 * TILE], ACT.Copy).then_inc(s_xrt[par], 1)

            def expert_biases(n, par):
                return act.value_load(tile_ex[0:1, bass.ds(n * 2 + par, 1)], min_val=0, max_val=E - 1) * FC

            load_table(GELU_TABLE)
            eng.wait_ge(s_wlo, NG)
            eng.wait_ge(s_routed, 1)
            for s in range(2):
                gelu(s, s, 2 * T, (E + s) * FC)
            with eng.Fori(1, SJA) as j:
                for s in range(2):
                    gelu(j * 2 + s, s, 2 * T, (E + s) * FC)
            for par in range(2):
                xr_out(0, par)
            with eng.Fori(0, NTILES // 2 - 1) as n:
                for par in range(2):
                    gelu(n * 2 + par + 2 * SJA, par, TILE, expert_biases(n, par))
                    xr_out(n + 1, par)
            for par in range(2):
                gelu(NTILES - 2 + par + 2 * SJA, par, TILE, expert_biases(NTILES // 2 - 1, par))
            with eng.Fori(SJA, SJ) as j:
                for s in range(2):
                    gelu(j * 2 + s + NTILES, s, 2 * T, (E + s) * FC)

        @block.vector
        def _(dve):
            eng = dve
            chain = [0]

            def link(ins):
                chain[0] += 1
                ins.then_inc(s_scale, 1)
                dve.wait_ge(s_scale, chain[0])

            eng.wait_ge(s_setup, 16 * N_SETUP)
            eng.wait_ge(s_w32, 16 * 4)
            for n, src in enumerate((w32[:, 0, :], b1[:], w32[:, 1, :], gatew[:])):
                nc.vector.tensor_reduce(mx[:, n:n + 1], src, X, ALU.max, apply_absolute_value=True).then_inc(s_mx, 1)
            eng.wait_ge(s_mxall, 1)
            link(nc.vector.scalar_tensor_tensor(mxall[:, 1:2], mxall[:, 0:1], float(D), mxall[:, 1:2], ALU.mult, ALU.add))
            link(nc.vector.tensor_scalar(mxall[:], mxall[:], LEAST, None, ALU.max))
            link(nc.vector.tensor_scalar(pw[:].bitcast(I32), mxall[:].bitcast(I32), TOPBITS, None, ALU.bitwise_and))
            link(nc.vector.reciprocal(up[:], pw[:]))
            link(nc.vector.tensor_scalar(up[:], up[:], LIFT, None, ALU.mult))
            link(nc.vector.tensor_scalar(down[:], pw[:], 1.0 / LIFT, None, ALU.mult))
            link(nc.vector.tensor_tensor(yscale[:], down[:, 1:2], down[:, 2:3], ALU.mult))
            link(nc.vector.tensor_tensor(rowb[:, 3, :], rowb[:, 3, :], rowb[:, 4, :], ALU.add))
            nc.vector.tensor_scalar(gsplit[:, 0], gatew[:], up[:, 3:4], None, ALU.mult).then_inc(s_gs, 1)
            eng.wait_ge(s_gs, 1)
            nc.vector.scalar_tensor_tensor(gsplit[:, 1], gatew[:], up[:, 3:4], gsplit[:, 0], ALU.mult, ALU.subtract).then_inc(s_gs, 1)

            def rows(g):
                return h_all[0:T, bass.ds(g * GROUP, GROUP), :]

            def stats(g, src, st, mv, s_a, s_done, s_before):
                done_apart(eng, s_before, g)
                for b in range(GROUP):
                    last = nc.vector.bn_stats(st[0:T, b, :], src[:, b, :])
                last.then_inc(s_a, 1)
                done_apart(eng, s_a, g + 1)
                for b in range(GROUP):
                    last = nc.vector.bn_aggr(mv[0:T, b, :], st[0:T, b, :])
                last.then_inc(s_done, 1)

            def h_out(g):
                done(eng, s_h_mm, g + 1)
                nc.vector.tensor_tensor(rows(g), h_ps[0:T, 0:GROUP * D].rearrange("p (b n) -> p b n", n=D),
                                        rowb[0:T, 0:1, :].to_broadcast([T, GROUP, D]), ALU.add).then_inc(s_h, 1)
                done_apart(eng, s_h, g + 1)
                stats(g, rows(g), st1, mv1, s_st1a, s_st1, s_ln)

            def ln_out(g):
                done(eng, s_t1, g)
                done(eng, s_rs1, g + 1)
                for b in range(GROUP):
                    last = nc.vector.tensor_scalar(ln[0:T, b, :], h_all[0:T, bass.ds(g * GROUP + b, 1), :].rearrange("p b n -> p (b n)"),
                                                   mv1[0:T, b, 0:1], rs1[0:T, b:b + 1], ALU.subtract, ALU.mult)
                last.then_inc(s_ln, 1)

            def rope_parts(g):
                done(eng, s_rope, g)
                done(eng, s_qk, g + 1)
                for n, src in enumerate((q_ps, qs_ps, k_ps, ks_ps)):
                    last = nc.vector.scalar_tensor_tensor(
                        rparts[:, n].rearrange("p (b t) -> p b t", t=T), src[:, 0:GT].rearrange("p (b t) -> p b t", t=T),
                        colb[:, n:n + 1], rope[:, n:n + 1, :].to_broadcast([P, GROUP, T]), ALU.add, ALU.mult)
                last.then_inc(s_rp, 1)

            def v_out(g):
                done(eng, s_pv, g)
                done(eng, s_v_mm, g + 1)
                nc.vector.tensor_tensor(v_tok[0:T], v_ps[0:T, 0:GROUP * D].rearrange("p (b n) -> p b n", n=D),
                                        rowb[0:T, 1:2, :].to_broadcast([T, GROUP, D]), ALU.add).then_inc(s_v, 1)

            def weights(g):
                done(eng, s_pv, g)
                done(eng, s_lnp, g + 1)
                nc.vector.scalar_tensor_tensor(wei[0:T], s_ps[0:T, 0:GT], 0.0, sp[0:T], ALU.max, ALU.add).then_inc(s_wei, 1)

            def h2_out(g):
                done(eng, s_hb, g + 1)
                done(eng, s_wp, g + 1)
                nc.vector.tensor_tensor(rows(g), wp_ps[0:T, 0:GROUP * D].rearrange("p (b n) -> p b n", n=D), rows(g),
                                        ALU.add).then_inc(s_h2, 1)
                done_apart(eng, s_h2, g + 1)
                stats(g, rows(g), st2, mv2, s_st2a, s_st2, s_xn)

            def x_out(g):
                done(eng, s_xlo, g)
                done(eng, s_rs2, g + 1)
                for b in range(GROUP):
                    last = nc.vector.tensor_scalar(xn[0:T, b, :], h_all[0:T, bass.ds(g * GROUP + b, 1), :].rearrange("p b n -> p (b n)"),
                                                   mv2[0:T, b, 0:1], rs2[0:T, b:b + 1], ALU.subtract, ALU.mult)
                last.then_inc(s_xn, 1)
                done(eng, s_t2, g)
                done(eng, s_xtok, g, 16)
                done(eng, s_xn, g + 1)
                nc.vector.tensor_copy(xsplit[0:T, :, 0, :], xn[0:T]).then_inc(s_xhi, 1)
                done(eng, s_xhi, g + 1)
                nc.vector.tensor_tensor(xsplit[0:T, :, 1, :], xn[0:T], xsplit[0:T, :, 0, :], ALU.subtract).then_inc(s_xlo, 1)

            def w_low(g):
                done(eng, s_whi, g + 1)
                for n, scale in ((0, up[:, 0:1]), (1, up[:, 2:3])):
                    c = bass.ds(g * WSTEP, WSTEP)
                    last = nc.vector.scalar_tensor_tensor(wlo[:, n, c], w32[:, n, c], scale, whi[:, n, c], ALU.mult, ALU.subtract)
                last.then_inc(s_wlo, 1)

            pipeline(eng, [(h2_out, -1), (x_out, -1), (weights, 0), (rope_parts, 1), (h_out, 2), (v_out, 1), (ln_out, 2), (w_low, 0)])

            n_r = [0]

            def link_r(ins):
                n_r[0] += 1
                ins.then_inc(s_r, 1)
                dve.wait_ge(s_r, n_r[0])

            def over_e(v):
                return v.rearrange("p (b e) -> p b e", e=1).to_broadcast([T, B, E])

            def over_b(v):
                return v.rearrange("p (b e) -> p b e", b=1).to_broadcast([T, B, E])

            L, A, C = logits[0:T], ra[0:T], rc[0:T]
            v = [rvec[0:T, n, :] for n in range(4)]
            eng.wait_ge(s_lg, NG)
            link_r(nc.vector.tensor_tensor(L, L, over_b(gateb[0:T]), ALU.add))
            link_r(nc.vector.tensor_reduce(v[0], L, X, ALU.max))
            link_r(nc.vector.tensor_tensor(L, L, over_e(v[0]), ALU.subtract))
            eng.wait_ge(s_rexp, 1)
            link_r(nc.vector.tensor_reduce(v[1], A, X, ALU.add))
            link_r(nc.vector.reciprocal(v[2], v[1]))
            link_r(nc.vector.tensor_tensor(A, A, over_e(v[2]), ALU.mult))
            src = A
            for k in range(TOP):
                link_r(nc.vector.tensor_reduce(gatev[0:T, k], src, X, ALU.max))
                link_r(nc.vector.tensor_tensor(C, src, over_e(gatev[0:T, k]), ALU.is_equal))
                link_r(nc.vector.tensor_tensor(C, C, over_b(prefer_low[0:T]), ALU.mult))
                link_r(nc.vector.tensor_reduce(v[3], C, X, ALU.max))
                link_r(nc.vector.tensor_tensor(oh[0:T, k], over_b(prefer_low[0:T]), over_e(v[3]), ALU.is_equal))
                if k == 0:
                    link_r(nc.vector.scalar_tensor_tensor(C, oh[0:T, 0], -2.0, A, ALU.mult, ALU.add))
                    src = C
            nc.vector.tensor_tensor(chosen[0:T].rearrange("p (b e) -> p b e", e=E), oh[0:T, 0], oh[0:T, 1], ALU.add).then_inc(s_chosen, 1)
            eng.wait_ge(s_rank, 1)
            rank = y_ps[0:T, 0, :].rearrange("p (b e) -> p b e", e=E)
            total = y_ps[0:T, 1, :].rearrange("p (b e) -> p b e", e=E)
            for e in range(E):
                last = nc.vector.tensor_tensor_scan(run[0:T, e, :], ones64[0:T], total[:, :, e], 0.0, ALU.mult, ALU.add)
            link_r(last)
            link_r(nc.vector.tensor_tensor(A, run[0:T].rearrange("p e b -> p b e"), total, ALU.subtract))
            link_r(nc.vector.tensor_tensor(A, A, rank, ALU.add))
            full = cmp[0:T, 0:E * MAXT].rearrange("p (e n) -> p e n", e=E)
            link_r(nc.vector.tensor_copy(te[0:T, 0], run[0:T, :, B - 1]))
            link_r(nc.vector.tensor_tensor(full, te[0:T, 0].rearrange("p (e n) -> p e n", n=1).to_broadcast([T, E, MAXT]),
                                           tile_steps[0:T].rearrange("p (e n) -> p e n", e=1).to_broadcast([T, E, MAXT]), ALU.is_gt))
            link_r(nc.vector.tensor_reduce(te[0:T, 1], full, X, ALU.add))
            link_r(nc.vector.tensor_tensor_scan(te[0:T, 2], ones64[0:T, 0:E], te[0:T, 1], 0.0, ALU.mult, ALU.add))
            link_r(nc.vector.tensor_tensor(te[0:T, 3], te[0:T, 2], te[0:T, 1], ALU.subtract))
            link_r(nc.vector.tensor_scalar(te[0:T, 3], te[0:T, 3], float(TILE), None, ALU.mult))
            passed = cmp[0:1, 0:NTILES * (E - 1)].rearrange("p (n e) -> p n e", e=E - 1)
            link_r(nc.vector.tensor_tensor(passed, tile_ids[0:1].rearrange("p (n e) -> p n e", e=1).to_broadcast([1, NTILES, E - 1]),
                                           te[0:1, 2, 0:E - 1].rearrange("p (n e) -> p n e", n=1).to_broadcast([1, NTILES, E - 1]), ALU.is_ge))
            link_r(nc.vector.tensor_reduce(tile_exf[:], passed, X, ALU.add))
            link_r(nc.vector.tensor_copy(tile_ex[:], tile_exf[:]))
            link_r(nc.vector.tensor_tensor(A, A, over_b(te[0:T, 3]), ALU.add))
            for k in range(TOP):
                link_r(nc.vector.tensor_tensor(C, oh[0:T, k], A, ALU.mult))
                link_r(nc.vector.tensor_reduce(posf[0:T, :, k], C, X, ALU.add))
            nc.vector.tensor_copy(pos[0:T], posf[0:T]).then_inc(s_routed, 1)
            eng.wait_ge(s_routed, 1)

            def split(u, par, n):
                g = gel[:, par].rearrange("p (f n) -> p f n", f=FC)[:, :, 0:n]
                done(eng, s_y_mm, u - 1)
                done(eng, s_gelu, u + 1)
                nc.vector.tensor_scalar(hhi[:, par, :, 0:n], g, up[:, 1:2], None, ALU.mult).then_inc(s_hhi, 1)
                done(eng, s_hhi, u + 1)
                nc.vector.scalar_tensor_tensor(hlo[:, par, :, 0:n], g, up[:, 1:2], hhi[:, par, :, 0:n], ALU.mult, ALU.subtract).then_inc(s_hlo, 1)

            def add_shared(j, base):
                done(eng, s_y_mm, j * 2 + 2 + base)
                hj = h_all[0:T, bass.ds(j * 2, 2), :]
                nc.vector.scalar_tensor_tensor(hj, y_ps[0:T, :, 0:D], yscale[0:T], hj, ALU.mult, ALU.add).then_inc(s_ysh, 1)

            def tile_output(n, par):
                t = n * 2 + par
                e = dve.value_load(tile_ex[0:1, bass.ds(t, 1)], min_val=0, max_val=E - 1)
                done(eng, s_yst[par], n, 16)
                done(eng, s_y_mm, t + 1 + 2 * SJA)
                nc.vector.scalar_tensor_tensor(
                    y_out[:, par], y_ps[:, par, 0:SUB * D].rearrange("p (s n) -> p s n", n=D), yscale[:],
                    b2[:, bass.ds(e, 1), :].to_broadcast([P, SUB, D]), ALU.mult, ALU.add).then_inc(s_yr[par], 1)

            def combine(n, par):
                g = n * 2 + par
                done(eng, s_gat[par], n + 1, 16 * GROUP * TOP)
                for k in range(TOP):
                    for b in range(GROUP):
                        row = h_all[0:T, bass.ds(g * GROUP + b, 1), :].rearrange("p b n -> p (b n)")
                        last = nc.vector.scalar_tensor_tensor(
                            row, gat[0:T, par, b, k, :], gatev[0:T, k, bass.ds(g * GROUP + b, 1)], row, ALU.mult, ALU.add)
                    if k == 0:
                        last.then_inc(s_half, 1)
                        done(eng, s_half, g + 1)
                last.then_inc(s_comb[par], 1)

            for s in range(2):
                split(s, s, 2 * T)
            with eng.Fori(1, SJA) as j:
                split(j * 2, 0, 2 * T)
                add_shared(j - 1, 0)
                split(j * 2 + 1, 1, 2 * T)
            split(2 * SJA, 0, TILE)
            add_shared(SJA - 1, 0)
            split(2 * SJA + 1, 1, TILE)

            def routed_step(n):
                for par in range(2):
                    tile_output(n - 1, par)
                    split(n * 2 + par + 2 * SJA, par, TILE)
            routed_step(1)
            with eng.Fori(2, NTILES // 2) as n:
                routed_step(n)
            for par in range(2):
                tile_output(NTILES // 2 - 1, par)
                split(SJA * 2 + par + NTILES, par, 2 * T)
            with eng.Fori(SJA + 1, SJ) as j:
                split(j * 2 + NTILES, 0, 2 * T)
                add_shared(j - 1, NTILES)
                split(j * 2 + 1 + NTILES, 1, 2 * T)
            add_shared(SJ - 1, NTILES)
            eng.wait_ge(s_ysh, SJ)
            with eng.Fori(0, NG // 2) as n:
                for par in range(2):
                    combine(n, par)


def kernel(**inputs):
    import numpy as np
    import concourse.bacc as bacc
    from concourse.bass_utils import run_bass_kernel_spmd
    import ml_dtypes

    def arr(name):
        return np.asarray(inputs[name])

    def cols(v):
        return v.reshape(-1, 1)

    def on_all(v):
        return np.broadcast_to(v, (P,) + v.shape)

    swap = np.arange(D).reshape(-1, 2)[:, ::-1].reshape(-1)
    where = np.arange(T - 1, -1, -1, dtype=np.float32)
    angle = (where[None, :] * np.arange(D // 2, dtype=np.float32)[:, None]).astype(np.float64)
    cos = np.repeat(np.cos(angle), 2, axis=0)
    sin = np.repeat(np.sin(angle), 2, axis=0) * np.tile([-1.0, 1.0], D // 2)[:, None]
    q_scale = float(D) ** -0.5
    rope = np.stack([cos * q_scale, sin * q_scale, cos, sin], axis=1).astype(np.float32)
    eye = np.eye(P)
    masked = np.where(np.arange(P)[None, :] < np.arange(P)[:, None], -1e30, 0.0)
    earlier = (np.arange(P)[:, None] < np.arange(P)[None, :]).astype(np.float32)
    counts = np.concatenate([np.arange(MAXT) * TILE, np.arange(NTILES), E - np.arange(E), np.zeros(E)]).astype(np.float32)

    wq, wk, bq, bk = arr("L0_attn_Wq"), arr("L0_attn_Wk"), arr("L0_attn_bq"), arr("L0_attn_bk")
    arrays = {
        "x": arr("x").reshape(B * T, CTX, D).transpose(2, 1, 0),
        "wt": arr("L0_tok_weight").reshape(D, CTX, D).transpose(2, 1, 0),
        "wmat": np.stack([wq, wq[:, swap], wk, wk[:, swap], arr("L0_attn_Wv"), arr("L0_attn_Wp")], axis=1),
        "rope": rope,
        "colb": np.concatenate([cols(bq), cols(bq[swap]), cols(bk), cols(bk[swap])], axis=1),
        "rowb": on_all(np.stack([arr("L0_tok_bias"), arr("L0_attn_bv"), arr("L0_attn_bp"),
                                 arr("L0_ffn_sb2")[0], arr("L0_ffn_sb2")[1]])),
        "gateb": on_all(arr("L0_ffn_gate_b")),
        "gatew": arr("L0_ffn_gate_w").T,
        "rb1": arr("L0_ffn_rb1").reshape(E * FC, P).T,
        "sb1": arr("L0_ffn_sb1").reshape(NS * FC, P).T,
        "rb2": on_all(arr("L0_ffn_rb2")),
        "rw1": arr("L0_ffn_rw1").transpose(2, 0, 1).reshape(D, E * F),
        "sw1": arr("L0_ffn_sw1").transpose(2, 0, 1).reshape(D, NS * F),
        "rw2": arr("L0_ffn_rw2").reshape(E, D, FC, P).transpose(3, 0, 2, 1).reshape(P, E * F),
        "sw2": arr("L0_ffn_sw2").reshape(NS, D, FC, P).transpose(3, 0, 2, 1).reshape(P, NS * F),
        "ident": eye.astype(np.float32),
        "identh": eye.astype(np.float16),
        "maskl": np.stack([eye, masked], axis=1).astype(ml_dtypes.bfloat16),
        "tri": np.stack([earlier, np.ones((P, P), np.float32)], axis=1).astype(ml_dtypes.bfloat16),
        "counts": on_all(counts),
    }
    arrays = {k: np.ascontiguousarray(v) for k, v in arrays.items()}
    nc = bacc.Bacc("TRN2", target_bir_lowering=False, num_devices=1)
    d = {k: nc.dram_tensor(f"in_{k}", v.shape, mybir.dt.from_np(v.dtype), kind="ExternalInput").ap() for k, v in arrays.items()}
    out = nc.dram_tensor("out", [B, T, D], F32, kind="ExternalOutput").ap()
    build(nc, d, out)
    r = run_bass_kernel_spmd(nc, [{f"in_{k}": v for k, v in arrays.items()}], core_ids=[0])
    return r.results[0]["out"]
```

```python
from contextlib import ExitStack

import concourse.bass as bass
from concourse import mybir

F32 = mybir.dt.float32
F16 = mybir.dt.float16
BF16 = mybir.dt.bfloat16
I32 = mybir.dt.int32
ALU = mybir.AluOpType
ACT = mybir.ActivationFunctionType
X = mybir.AxisListType.X
ABSMAX = bass.bass_isa.ReduceOp.max

P = 128
B = 64
T = 125
CTX = 3
D = 128
E = 8
NS = 2
NE = E + NS
F = 512
FC = F // P
TOP = 2
EPS = 1e-5
GROUP = 4
NG = B // GROUP
GT = GROUP * T
TILE = 256
SUB = TILE // P
HALVES = 2
HB = B // HALVES
HG = NG // HALVES
SLOTS_USED = HB * T * TOP
HTILES = (SLOTS_USED + E * (TILE - 1)) // TILE
HTILES += HTILES % 2
NTILES = HALVES * HTILES
SLOTS = NTILES * TILE
MAXT = -(-HB * T // TILE)
SJ = B // 2
SJA = 4
WCOLS = NE * F
WSTEP = WCOLS // HG
TOPBITS = 0x7F800000
SCATTERS_PER_STEP = 1
ZROWS = 2
EXP_LN_TABLE = 6
GELU_TABLE = 10
LIFT = 2.0 ** 14
LEAST = 2.0 ** -40


def build(nc, d, out):
    x_tok = nc.dram_tensor("x_tok", [B * T, 2 * D], F16).ap()
    x_slots = nc.dram_tensor("x_slots", [SLOTS, 2 * D], F16).ap()
    y_slots = nc.dram_tensor("y_slots", [SLOTS, D], F32).ap()

    with ExitStack() as ctx:
        def sb(name, shape, dt):
            return ctx.enter_context(nc.sbuf_tensor(name, shape, dt))

        def psum(name, shape, dt):
            return ctx.enter_context(nc.psum_tensor(name, shape, dt))

        def sem(name):
            return ctx.enter_context(nc.semaphore(name))

        pre_ps = psum("pre_ps", [P, 2, 2, 512], F32)
        xp_ps = psum("xp_ps", [P, 2, 512], F32)
        y_ps = psum("y_ps", [P, 2, 512], F32)
        q_ps, qs_ps = pre_ps[:, 0, 0, :], pre_ps[:, 0, 1, :]
        k_ps, ks_ps = pre_ps[:, 1, 0, :], pre_ps[:, 1, 1, :]
        v_ps, wp_ps = q_ps, qs_ps
        s_ps, t1_ps = xp_ps[:, 0, :], xp_ps[:, 1, :]
        lg_ps = t1_ps
        t2_ps, h_ps = y_ps[:, 0, :], y_ps[:, 1, :]
        pv_ps = rank_ps = t2_ps

        wt = sb("wt", [P, CTX, D], F32)
        wmat = sb("wmat", [P, 6, D], F32)
        rope = sb("rope", [P, 4, T], F32)
        colb = sb("colb", [P, 4], F32)
        rowb = sb("rowb", [P, 5, D], F32)
        gateb = sb("gateb", [P, E], F32)
        ident = sb("ident", [P, P], F32)
        identh = sb("identh", [P, P], F16)
        maskl = sb("maskl", [P, 2, P], BF16)
        tri = sb("tri", [P, 2, P], BF16)
        counts_const = sb("counts_const", [P, MAXT + HTILES + E], F32)
        tile_steps = counts_const[:, 0:MAXT]
        tile_ids = counts_const[:, MAXT:MAXT + HTILES]
        prefer_low = counts_const[:, MAXT + HTILES:]
        gatew = sb("gatew", [P, E], F32)
        b1 = sb("b1", [P, NE * FC], F32)
        b2 = sb("b2", [P, E, D], F32)
        epsc = sb("epsc", [P, 2, GROUP], F32)
        ones64 = sb("ones64", [P, B], F32)
        zeros = sb("zeros", [P, ZROWS * 2 * D], F16)
        w32 = sb("w32", [P, 2, WCOLS], F32)
        whi = sb("whi", [P, 2, WCOLS], F16)
        wlo = sb("wlo", [P, 2, WCOLS], F16)
        gsplit = sb("gsplit", [P, 2, E], F16)
        mx = sb("mx", [P, 4], F32)
        mxall = sb("mxall", [P, 4], F32)
        pw = sb("pw", [P, 4], F32)
        up = sb("up", [P, 4], F32)
        down = sb("down", [P, 4], F32)
        yscale = sb("yscale", [P, 1], F32)

        flow = sb("flow", [P, 16 * 512], F32)
        taken = [0]

        def carve(n):
            taken[0] += n
            assert taken[0] <= 16 * 512
            return flow[:, taken[0] - n:taken[0]]

        x_in = carve(CTX * GT).rearrange("p (c n) -> p c n", c=CTX)
        h_all = sb("h_all", [P, B, D], F32)
        st1 = sb("st1", [P, GROUP, 6], F32)
        mv1 = sb("mv1", [P, GROUP, 2], F32)
        rs1 = sb("rs1", [P, GROUP], F32)
        ve1 = sb("ve1", [P, GROUP], F32)
        ln = carve(GROUP * D).rearrange("p (b n) -> p b n", b=GROUP)
        ln_t = carve(GT)
        rparts = carve(4 * GT).rearrange("p (a n) -> p a n", a=4)
        q_t = carve(GT)
        k_t = carve(GT)
        v_tok = carve(GROUP * D).rearrange("p (b n) -> p b n", b=GROUP)
        sp = carve(GT)
        wei = carve(GT)
        att_t = carve(GT)
        st2 = sb("st2", [P, GROUP, 6], F32)
        mv2 = sb("mv2", [P, GROUP, 2], F32)
        rs2 = sb("rs2", [P, GROUP], F32)
        ve2 = sb("ve2", [P, GROUP], F32)
        xn = carve(GROUP * D).rearrange("p (b n) -> p b n", b=GROUP)
        xsplit = sb("xsplit", [P, GROUP, 2, D], F16)
        xt_all = sb("xt_all", [P, 2, B * T], F16)
        logits = sb("logits", [P, B, E], F32)

        chosen = sb("chosen", [P, HB * E], BF16)
        rvec = sb("rvec", [P, 4, HB], F32)
        gatev = sb("gatev", [P, TOP, B], F32)
        te = sb("te", [P, 4, E], F32)
        posf = sb("posf", [P, HB, TOP], F32)
        pos = sb("pos", [P, B, TOP], I32)
        tile_exf = sb("tile_exf", [1, HTILES], F32)
        tile_ex = sb("tile_ex", [1, NTILES // 2 + 2, 4], I32)

        w32f = w32[:, :, :].rearrange("p a n -> p (a n)")
        gel = w32f[:, 0:2 * FC * TILE].rearrange("p (b n) -> p b n", b=2)
        o = 2 * FC * TILE
        rows_a = w32f[:, o:o + HB * D].bitcast(F16).rearrange("p (b n) -> p b n", b=HB)
        gat = w32f[:, o:o + 2 * GROUP * TOP * D].rearrange("p (b g k n) -> p b g k n", b=2, g=GROUP, k=TOP)
        o += HB * D
        cmp = w32f[:, o:o + 512]
        o += 512
        ra, rc = (w32f[:, o + n * HB * E:o + (n + 1) * HB * E].rearrange("p (b e) -> p b e", e=E) for n in range(2))
        o += 2 * HB * E
        oh = w32f[:, o:o + TOP * HB * E].rearrange("p (k b e) -> p k b e", k=TOP, e=E)
        o += TOP * HB * E
        run = w32f[:, o:o + HB * E].rearrange("p (e b) -> p e b", e=E)
        o += HB * E
        hhi, hlo = (w32f[:, o + n * FC * TILE:o + (n + 1) * FC * TILE].bitcast(F16)
                    .rearrange("p (b f n) -> p b f n", b=2, f=FC) for n in range(2))
        o += 2 * FC * TILE
        assert o <= 2 * WCOLS
        xr_t = sb("xr_t", [P, 2, 2, TILE], F16)
        rows_b = flow[:, 0:HB * D].bitcast(F16).rearrange("p (b n) -> p b n", b=HB)
        o = HB * D
        xr_in = flow[:, o:o + 2 * SUB * D].bitcast(F16).rearrange("p (b s n) -> p b s n", b=2, s=SUB)
        o += 2 * SUB * D
        y_out = flow[:, o:o + 2 * SUB * D].rearrange("p (b s n) -> p b s n", b=2, s=SUB)
        srow = sb("srow", [P, 2, 2 * D], F16)
        sidx = sb("sidx", [P, 2, TOP], I32)
        gidx = sb("gidx", [P, 2, GROUP, TOP], I32)
        s_setup = sem("setup_loaded")
        s_w32 = sem("weights_loaded")
        s_const = sem("consts_set")
        s_zero = sem("slots_zeroed")
        s_mx = sem("maxima_taken")
        s_mxall = sem("maxima_joined")
        s_scale = sem("scales_chain")
        s_gs = sem("gate_split")
        s_x = sem("x_loaded")
        s_h_mm = sem("h_products")
        s_h = sem("h_stored")
        s_st1a, s_st1, s_ve1, s_rs1, s_ln = (sem(n) for n in ("ln1_stats", "ln1_moments", "ln1_var_eps", "ln1_rstd", "ln1_done"))
        s_t1, s_lnt = sem("ln1_transposed"), sem("ln1_t_stored")
        s_qk, s_rp, s_rope = sem("qk_products"), sem("rope_parts"), sem("rope_done")
        s_v_mm, s_v = sem("v_products"), sem("v_stored")
        s_s, s_abs, s_exp, s_lnp, s_wei = (sem(n) for n in ("scores", "score_abs", "score_exp", "score_log", "weights_done"))
        s_pv, s_att, s_wp, s_hb, s_h2 = (sem(n) for n in ("pv_products", "att_stored", "wp_products", "h_plus_bp", "h2_done"))
        s_st2a, s_st2, s_ve2, s_rs2, s_xn = (sem(n) for n in ("ln2_stats", "ln2_moments", "ln2_var_eps", "ln2_rstd", "ln2_done"))
        s_xhi, s_xlo, s_xtok, s_hb2 = (sem(n) for n in ("x_high", "x_low", "x_tok_stored", "h2_plus_b2"))
        s_t2, s_xt, s_lg_mm, s_lg = (sem(n) for n in ("x_transposed", "x_t_stored", "gate_products", "logits_stored"))
        s_whi, s_wlo = sem("w_high"), sem("w_low")
        s_r = sem("routing_chain")
        s_centred, s_rexp = sem("logits_centred"), sem("router_exp")
        s_rank, s_rank_read = sem("rank_products"), sem("ranks_read")
        s_routed = sem("routing_done")
        s_chosen = sem("experts_chosen")
        s_rows = [sem(f"half{h}_rows_loaded") for h in range(HALVES)]
        s_stage, s_gidx = sem("batch_staged"), sem("gather_indices_staged")
        s_scat = [sem(f"scattered{p}") for p in range(2)]
        s_xr = [sem(f"tile_loaded{p}") for p in range(2)]
        s_xp = [sem(f"tile_transposed{p}") for p in range(2)]
        s_xrt = [sem(f"tile_t_stored{p}") for p in range(2)]
        s_pre = [sem(f"pre_half{p}") for p in range(2)]
        s_gelu, s_hhi, s_hlo = sem("gelu_done"), sem("hidden_high"), sem("hidden_low")
        s_y_mm, s_ysh = sem("unit_outputs"), sem("shared_added")
        s_yr = [sem(f"tile_output{p}") for p in range(2)]
        s_yst = [sem(f"tile_stored{p}") for p in range(2)]
        s_gat = [sem(f"gathered{p}") for p in range(2)]
        s_half, s_out = sem("first_expert_added"), sem("out_stored")
        s_comb = [sem(f"experts_added{p}") for p in range(2)]

        block = ctx.enter_context(nc.Block())

        def done(eng, s, n, step=1):
            if isinstance(n, int):
                if n > 0:
                    eng.wait_ge(s, n * step)
            else:
                eng.wait_ge(s, n * step if step != 1 else n)

        def done_apart(eng, s, n, step=1):
            if isinstance(n, int):
                done(eng, s, n, step)
            else:
                value = eng.to_reg(n * step if step != 1 else n)
                eng.wait_ge(s_const, 1)
                eng.wait_ge(s, value)

        def upto(n):
            return min(n, NG) if isinstance(n, int) else n

        def pipeline(eng, stages, midway):
            stages = [(s[0], s[1], s[2] if len(s) > 2 else range(NG)) for s in stages]
            first = min(r.start - lag for _, lag, r in stages)
            last = max(r.stop - 1 - lag for _, lag, r in stages)
            lo = max(-lag for _, lag, _ in stages) + 1
            hi = min(NG - lag for _, lag, _ in stages)
            mid = HG + 1

            def step(i, where):
                for stage, lag, r in stages:
                    if where + lag in r:
                        stage(i + lag)

            for i in range(first, lo):
                step(i, i)
            with eng.Fori(lo, mid - 1) as i:
                step(i, lo)
            step(mid - 1, mid - 1)
            midway()
            with eng.Fori(mid, hi) as i:
                step(i, mid)
            for i in range(hi, last + 1):
                step(i, i)

        N_SETUP = 15

        segments = [("shared", SJA, 0), ("routed", NTILES // 2, 0), ("shared", SJ - SJA, SJA)]

        def run_units(eng, step, unroll=1):
            starts = [sum(pairs for _, pairs, _ in segments[:m]) for m in range(len(segments))]
            total = starts[-1] + segments[-1][1]

            def at(p):
                def pair(k):
                    for (kind, pairs, first), start in zip(segments, starts):
                        if start <= p + k < start + pairs:
                            return kind, p + k - start + first
                    return None, 0
                return pair

            def step_in_loop(kind, i, c, local):
                step(i * unroll + c, lambda k: (kind, i * unroll + (local + k)), i, c)

            p = -2
            for (kind, pairs, first), start in zip(segments, starts):
                while p < start + 2:
                    step(p, at(p), 0, p)
                    p += 1
                turns = (pairs - 4) // unroll
                if turns > 0:
                    with eng.Fori(0, turns) as i:
                        for c in range(start + 2, start + 2 + unroll):
                            step_in_loop(kind, i, c, c - start + first)
                    p += turns * unroll
            while p < total:
                step(p, at(p), 0, p)
                p += 1

        def experts_of(engine, n, lo, hi):
            _, values = nc.values_load_multi_w_load_instructions(
                tile_ex[0:1, bass.ds(n + 2, 1), lo:hi].rearrange("p n k -> p (n k)"), engines=[engine],
                min_val=0, max_val=E - 1,
                skip_runtime_bounds_check_because="a count of passed boundaries between E experts is at most E - 1")
            return values

        @block.sync
        def _(sp_eng):
            eng = sp_eng
            loads = [(wt[:], d["wt"]), (rowb[:], d["rowb"]), (ident[:], d["ident"]), (wmat[:], d["wmat"]),
                     (rope[:], d["rope"]), (colb[:], d["colb"]), (maskl[:], d["maskl"]), (identh[:], d["identh"]),
                     (gateb[:], d["gateb"]), (gatew[:], d["gatew"]), (tri[:], d["tri"]),
                     (counts_const[:], d["counts"]), (b1[:, 0:E * FC], d["rb1"]), (b1[:, E * FC:], d["sb1"]),
                     (b2[:], d["rb2"])]
            assert len(loads) == N_SETUP
            x_d = d["x"]

            def load_x(g):
                done(eng, s_h_mm, g)
                eng.dma_start(x_in, x_d[:, :, bass.ds(g * GT, GT)]).then_inc(s_x, 16)

            def store_x_tok(g):
                done_apart(eng, s_xlo, g + 1)
                eng.dma_start(x_tok[bass.ds(g * GT, GT), :].rearrange("(b t) n -> t b n", t=T),
                              xsplit[0:T].rearrange("p b h n -> p b (h n)")).then_inc(s_xtok, 16)

            for n, (dst, src) in enumerate(loads):
                eng.dma_start(dst, src).then_inc(s_setup, 16)
                if n == 1:
                    load_x(0)
            eng.dma_start(w32[:, 0, 0:E * F], d["rw1"]).then_inc(s_w32, 16)
            eng.dma_start(w32[:, 0, E * F:], d["sw1"]).then_inc(s_w32, 16)
            eng.dma_start(w32[:, 1, 0:E * F], d["rw2"]).then_inc(s_w32, 16)
            eng.dma_start(w32[:, 1, E * F:], d["sw2"]).then_inc(s_w32, 16)
            eng.wait_ge(s_const, 3)
            rows = SLOTS // P // ZROWS
            eng.dma_start(x_slots.rearrange("(p a r) n -> p a (r n)", p=P, a=rows),
                          zeros[:].rearrange("p (a n) -> p a n", a=1).to_broadcast([P, rows, ZROWS * 2 * D])
                          ).then_inc(s_zero, 16)
            for g in range(1, 4):
                load_x(g)
            with eng.Fori(4, HG + 4) as g:
                load_x(g)
                store_x_tok(g - 4)

            def load_rows(dst, h):
                eng.wait_ge(s_xtok, 16 * HG * (h + 1))
                eng.dma_start(dst[0:T], x_tok[h * HB * T:(h + 1) * HB * T, :].rearrange("(b t) n -> t b n", t=T)
                              ).then_inc(s_rows[h], 16)
            load_x(HG + 4)
            eng.wait_ge(s_wlo, HG)
            load_rows(rows_a, 0)
            store_x_tok(HG)
            with eng.Fori(HG + 5, NG) as g:
                load_x(g)
                store_x_tok(g - 4)
            for g in range(NG - 4, NG):
                store_x_tok(g)
            load_rows(rows_b, 1)

            def wait_scattered(h):
                for par in range(2):
                    eng.wait_ge(s_scat[par], 16 * TOP * HB // 2 * (h + 1))

            def load_tile(n, par):
                done_apart(eng, s_xp[par], n)
                eng.dma_start(xr_in[:, par], x_slots[bass.ds((n * 2 + par) * TILE, TILE), :]
                              .rearrange("(s p) n -> p s n", p=P)).then_inc(s_xr[par], 16)

            def store_tile(n, par):
                done_apart(eng, s_yr[par], n + 1)
                eng.dma_start(y_slots[bass.ds((n * 2 + par) * TILE, TILE), :]
                              .rearrange("(s p) n -> p s n", p=P), y_out[:, par]).then_inc(s_yst[par], 16)
            wait_scattered(0)
            for n in range(3):
                for par in range(2):
                    load_tile(n, par)
            with eng.Fori(3, HTILES // 2) as n:
                for par in range(2):
                    load_tile(n, par)
                    store_tile(n - 3, par)
            wait_scattered(1)
            with eng.Fori(HTILES // 2, NTILES // 2) as n:
                for par in range(2):
                    load_tile(n, par)
                    store_tile(n - 3, par)
            for n in range(NTILES // 2 - 3, NTILES // 2):
                for par in range(2):
                    store_tile(n, par)

            with eng.Fori(0, NG // 2) as n:
                for par in range(2):
                    g = n * 2 + par
                    done_apart(eng, s_comb[par], n + 1)
                    eng.dma_start(out[bass.ds(g * GROUP, GROUP)].rearrange("b t n -> t b n"),
                                  h_all[0:T, bass.ds(g * GROUP, GROUP), :]).then_inc(s_out, 16)
            eng.wait_ge(s_out, 16 * NG)
            eng.wait_ge(s_zero, 16)

        @block.gpsimd
        def _(pool):
            eng = pool
            nc.gpsimd.memset(epsc[:, 0], EPS)
            nc.gpsimd.memset(epsc[:, 1], -0.5)
            nc.gpsimd.memset(ones64[:], 1.0).then_inc(s_const, 1)
            nc.gpsimd.memset(zeros[:], 0.0).then_inc(s_const, 2)
            eng.wait_ge(s_const, 3)
            eng.wait_ge(s_mx, 4)
            nc.gpsimd.partition_all_reduce(mxall[:], mx[:], P, ABSMAX).then_inc(s_mxall, 1)

            def rstd1(g):
                done(eng, s_st1, g + 1)
                nc.gpsimd.tensor_tensor(ve1[0:T], mv1[0:T, :, 1], epsc[0:T, 0], ALU.add).then_inc(s_ve1, 1)
                done(eng, s_ve1, g + 1)
                nc.gpsimd.tensor_tensor(rs1[0:T], ve1[0:T], epsc[0:T, 1], ALU.pow).then_inc(s_rs1, 1)

            def add_bp(g):
                done(eng, s_ln, g + 1)
                hg = h_all[0:T, bass.ds(g * GROUP, GROUP), :]
                nc.gpsimd.tensor_tensor(hg, hg, rowb[0:T, 2:3, :].to_broadcast([T, GROUP, D]), ALU.add).then_inc(s_hb, 1)

            def rope_add(g):
                done(eng, s_s, g)
                done(eng, s_rp, g + 1)
                nc.gpsimd.tensor_tensor(q_t, rparts[:, 0], rparts[:, 1], ALU.add)
                nc.gpsimd.tensor_tensor(k_t, rparts[:, 2], rparts[:, 3], ALU.add).then_inc(s_rope, 1)

            def rstd2(g):
                done(eng, s_st2, g + 1)
                nc.gpsimd.tensor_tensor(ve2[0:T], mv2[0:T, :, 1], epsc[0:T, 0], ALU.add).then_inc(s_ve2, 1)
                done(eng, s_ve2, g + 1)
                nc.gpsimd.tensor_tensor(rs2[0:T], ve2[0:T], epsc[0:T, 1], ALU.pow).then_inc(s_rs2, 1)

            def add_b2(g):
                done(eng, s_xn, g + 1)
                hg = h_all[0:T, bass.ds(g * GROUP, GROUP), :]
                nc.gpsimd.tensor_tensor(hg, hg, rowb[0:T, 3:4, :].to_broadcast([T, GROUP, D]), ALU.add).then_inc(s_hb2, 1)

            def scatter(n):
                half = 0 if scatter_half[0] == 0 else 1
                rows = (rows_a, rows_b)[half]
                for par in range(2):
                    done_apart(eng, s_scat[par], n, 16 * TOP)
                    nc.gpsimd.tensor_copy(sidx[0:T, par], pos[0:T, bass.ds(n * 2 + par, 1), :].rearrange("p b k -> p (b k)")).then_inc(s_stage, 1)
                    nc.gpsimd.tensor_copy(srow[0:T, par].bitcast(F32), rows[0:T, bass.ds(n * 2 + (par - half * HB), 1), :].rearrange("p b n -> p (b n)").bitcast(F32)).then_inc(s_stage, 1)
                for par in range(2):
                    done_apart(eng, s_stage, n * 2 + (par + 1), 2)
                    for k in range(TOP):
                        nc.gpsimd.indirect_dma_start(
                            x_slots, bass.IndirectOffsetOnAxis(ap=sidx[0:T, par, k:k + 1], axis=0),
                            srow[0:T, par], None).then_inc(s_scat[par], 16)
            scatter_half = [0]

            def gather(n, par):
                done_apart(eng, s_gat[par], n, 16 * GROUP * TOP)
                done_apart(eng, s_comb[par], n)
                nc.gpsimd.tensor_copy(gidx[0:T, par], pos[0:T, bass.ds((n * 2 + par) * GROUP, GROUP), :]).then_inc(s_gidx, 1)
                done_apart(eng, s_gidx, n * 2 + par + 1)
                for b in range(GROUP):
                    for k in range(TOP):
                        nc.gpsimd.indirect_dma_start(
                            gat[0:T, par, b, k, :], None,
                            y_slots, bass.IndirectOffsetOnAxis(ap=gidx[0:T, par, b, k:k + 1], axis=0),
                        ).then_inc(s_gat[par], 16)

            def start_scatter():
                eng.wait_ge(s_routed, 1)
                eng.wait_ge(s_zero, 16)
                eng.wait_ge(s_rows[0], 16)
                scatter(0)

            per_step = SCATTERS_PER_STEP

            def scatter_some(i):
                for m in range(per_step):
                    scatter((i - (HG + 1)) * per_step + (1 + m))

            steps = range(HG + 1, NG + 1)
            pipeline(eng, [(rstd2, -1), (rstd1, 2), (add_b2, -1), (rope_add, 1), (add_bp, 2), (scatter_some, 0, steps)], start_scatter)
            with eng.Fori(1 + len(steps) * per_step, HB // 2) as n:
                scatter(n)
            scatter_half[0] = 1
            eng.wait_ge(s_routed, 2)
            eng.wait_ge(s_rows[1], 16)
            with eng.Fori(HB // 2, B // 2) as n:
                scatter(n)

            for par in range(2):
                eng.wait_ge(s_yst[par], 16 * NTILES // 2)
            for par in range(2):
                gather(0, par)
            with eng.Fori(1, NG // 2) as n:
                for par in range(2):
                    gather(n, par)

        @block.tensor
        def _(pe):
            eng = pe

            def h_mm(g):
                done(eng, s_h, g)
                done(eng, s_x, g + 1, 16)
                for b in range(GROUP):
                    for c in range(CTX):
                        last = nc.tensor.matmul(h_ps[0:T, b * D:(b + 1) * D], x_in[:, c, b * T:(b + 1) * T], wt[:, c, :],
                                                start=(c == 0), stop=(c == CTX - 1))
                last.then_inc(s_h_mm, 1)

            def t1(g):
                done(eng, s_lg, g - 2)
                done(eng, s_lnt, g)
                done(eng, s_ln, g + 1)
                for b in range(GROUP):
                    last = nc.tensor.transpose(t1_ps[:, b * T:(b + 1) * T], ln[0:T, b, :], ident[0:T, 0:T])
                last.then_inc(s_t1, 1)

            def qk(g):
                done(eng, s_v, g)
                done(eng, s_h2, g - 1)
                done(eng, s_rp, g)
                done(eng, s_lnt, g + 1)
                for n, dst in enumerate((q_ps, qs_ps, k_ps, ks_ps)):
                    last = nc.tensor.matmul(dst[:, 0:GT], wmat[:, n, :], ln_t, start=True, stop=True)
                last.then_inc(s_qk, 1)

            def v_mm(g):
                done(eng, s_rp, g + 1)
                for b in range(GROUP):
                    last = nc.tensor.matmul(v_ps[0:T, b * D:(b + 1) * D], ln_t[:, b * T:(b + 1) * T], wmat[:, 4, :],
                                            start=True, stop=True)
                last.then_inc(s_v_mm, 1)

            def s_mm(g):
                done(eng, s_wei, g)
                done(eng, s_rope, g + 1)
                nc.tensor.matmul(s_ps[0:T, 0:GT], maskl[0:T, 0, 0:T],
                                 maskl[0:T, 1:2, 0:T].to_broadcast([T, GROUP, T]), start=True, stop=False)
                for b in range(GROUP):
                    c = slice(b * T, (b + 1) * T)
                    last = nc.tensor.matmul(s_ps[0:T, c], q_t[:, c], k_t[:, c], start=False, stop=(b == GROUP - 1))
                last.then_inc(s_s, 1)

            def pv(g):
                done(eng, s_xt, g - 1)
                done(eng, s_v, g + 1)
                done(eng, s_wei, g + 1)
                for b in range(GROUP):
                    c = slice(b * T, (b + 1) * T)
                    last = nc.tensor.matmul(pv_ps[:, c], v_tok[0:T, b, :], wei[0:T, c], start=True, stop=True)
                last.then_inc(s_pv, 1)

            def wp(g):
                done(eng, s_rp, upto(g + 2))
                done(eng, s_att, g + 1)
                for b in range(GROUP):
                    last = nc.tensor.matmul(wp_ps[0:T, b * D:(b + 1) * D], att_t[:, b * T:(b + 1) * T], wmat[:, 5, :],
                                            start=True, stop=True)
                last.then_inc(s_wp, 1)

            t2_h = t2_ps.bitcast(F16)

            def t2(g):
                done(eng, s_att, upto(g + 2))
                done(eng, s_xlo, g + 1)
                for h in range(2):
                    for b in range(GROUP):
                        c = h * 512 + b * P
                        last = nc.tensor.transpose(t2_h[:, c:c + T], xsplit[0:T, b, h, :], identh[0:T, 0:T])
                last.then_inc(s_t2, 1)

            def lg(g):
                done(eng, s_lnt, upto(g + 3))
                done(eng, s_gs, 2)
                done(eng, s_xt, g + 1)
                for b in range(GROUP):
                    xh = xt_all[:, 0, bass.ds(g * GT + b * T, T)]
                    xl = xt_all[:, 1, bass.ds(g * GT + b * T, T)]
                    dst = lg_ps[0:T, b * E:(b + 1) * E]
                    nc.tensor.matmul(dst, xh, gsplit[:, 0], start=True, stop=False)
                    nc.tensor.matmul(dst, xh, gsplit[:, 1], start=False, stop=False)
                    last = nc.tensor.matmul(dst, xl, gsplit[:, 0], start=False, stop=True)
                last.then_inc(s_lg_mm, 1)

            def ranks(h):
                eng.wait_ge(s_chosen, h + 1)
                eng.wait_ge(s_xt, HG * (h + 1))
                for n in range(2):
                    last = nc.tensor.matmul(rank_ps[0:T, n * HB * E:(n + 1) * HB * E], tri[0:T, n, 0:T], chosen[0:T], start=True, stop=True)
                last.then_inc(s_rank, 1)
                eng.wait_ge(s_rank_read, h + 1)

            eng.wait_ge(s_setup, 16 * N_SETUP)
            pipeline(eng, [(s_mm, 0), (t1, 1), (qk, 1), (pv, 0), (h_mm, 3), (t2, -1), (v_mm, 1), (wp, 0), (lg, -1)], lambda: ranks(0))

            ranks(1)

            w8 = [w[:, :, :].bitcast(mybir.dt.uint8) for w in (whi, wlo)]

            def part(w, k, col, f):
                return w8[w][:, k, bass.ds(col * 2 + f * 2 * P, 2 * P)].bitcast(F16)

            def unit_up(u, par, x_hi, x_lo, n, col):
                done(eng, s_gelu, u - 1)
                for f in range(FC):
                    dst = pre_ps[:, par, f // 2, (f % 2) * TILE:(f % 2) * TILE + n]
                    hi, lo = part(0, 0, col, f), part(1, 0, col, f)
                    nc.tensor.matmul(dst, hi, x_hi, start=True, stop=False)
                    nc.tensor.matmul(dst, hi, x_lo, start=False, stop=False)
                    last = nc.tensor.matmul(dst, lo, x_hi, start=False, stop=True)
                    if f % 2:
                        last.then_inc(s_pre[f // 2], 1)

            def unit_down(u, par, m, dsts, col, first, final):
                done(eng, s_hlo, u + 1)
                for t in range(2):
                    for f in range(FC):
                        h = hhi[:, par, f, t * m:(t + 1) * m]
                        l = hlo[:, par, f, t * m:(t + 1) * m]
                        hi, lo = part(0, 1, col, f), part(1, 1, col, f)
                        nc.tensor.matmul(dsts[t], h, hi, start=first and f == 0, stop=False)
                        nc.tensor.matmul(dsts[t], h, lo, start=False, stop=False)
                        last = nc.tensor.matmul(dsts[t], l, hi, start=False, stop=final and f == FC - 1)
                last.then_inc(s_y_mm, 1)

            xp_h = [xp_ps[:, p, :].bitcast(F16) for p in range(2)]

            def transpose_tile(n, par):
                done(eng, s_xrt[par], n)
                done(eng, s_xr[par], n + 1, 16)
                for h in range(2):
                    for s in range(SUB):
                        c = h * TILE + s * P
                        last = nc.tensor.transpose(xp_h[par][:, c:c + P], xr_in[:, par, s, h * D:(h + 1) * D], identh[:])
                last.then_inc(s_xp[par], 1)

            def up_step(u, kind, n, par, expert):
                if kind == "shared":
                    cols = bass.ds(n * 2 * T, 2 * T)
                    unit_up(u, par, xt_all[:, 0, cols], xt_all[:, 1, cols], 2 * T, (E + par) * F)
                if kind == "routed":
                    done(eng, s_xrt[par], n + 1)
                    unit_up(u, par, xr_t[:, par, 0], xr_t[:, par, 1], TILE, expert * F)

            def down_step(u, kind, n, par, expert):
                if kind == "shared":
                    if par == 0:
                        done(eng, s_ysh, n)
                        if isinstance(n, int) and n == SJA:
                            for p in range(2):
                                eng.wait_ge(s_yr[p], NTILES // 2)
                    unit_down(u, par, T, [y_ps[0:T, t, 0:D] for t in range(2)], (E + par) * F, par == 0, par == 1)
                if kind == "routed":
                    if isinstance(n, int) and n == 0:
                        eng.wait_ge(s_ysh, SJA)
                    done(eng, s_yr[par], n)
                    unit_down(u, par, P, [y_ps[:, par, s * D:(s + 1) * D] for s in range(SUB)], expert * F, True, True)

            def pe_step(p, pair, i, c):
                (kind0, n0), (kind1, n1), (kind2, n2) = pair(0), pair(1), pair(2)
                experts = [0] * 4
                if "routed" in (kind0, kind1, kind2):
                    n = n0 if kind0 == "routed" else n1 - 1 if kind1 == "routed" else n2 - 2
                    experts = experts_of(mybir.EngineType.PE, n, 0, 4)
                for par in range(2):
                    down_step(p * 2 + par, kind0, n0, par, experts[par])
                    if kind2 == "routed":
                        transpose_tile(n2, par)
                    if par == 0:
                        up_step(p * 2 + 3, kind1, n1, 1, experts[2])
                    else:
                        up_step(p * 2 + 4, kind2, n2, 0, experts[3])

            eng.wait_ge(s_wlo, HG)
            eng.wait_ge(s_xt, NG)
            eng.wait_ge(s_routed, 2)
            run_units(eng, pe_step)

        @block.scalar
        def _(act):
            eng = act

            def load_table(table):
                eng.add_instruction(mybir.InstLoadActFuncSet(
                    name=nc.get_next_instruction_name(), engine=mybir.EngineType.Activation, act_func_set_id=table))

            def softplus_abs(g):
                done(eng, s_s, g + 1)
                nc.scalar.activation(sp[0:T], s_ps[0:T, 0:GT], ACT.Abs).then_inc(s_abs, 1)

            def softplus_log(g):
                done(eng, s_abs, g + 1)
                nc.scalar.activation(sp[0:T], sp[0:T], ACT.Exp, scale=-1.0).then_inc(s_exp, 1)
                done(eng, s_exp, g + 1)
                nc.scalar.activation(sp[0:T], sp[0:T], ACT.Ln, bias=1.0).then_inc(s_lnp, 1)

            def ln_t_out(g):
                done(eng, s_v_mm, g)
                done(eng, s_t1, g + 1)
                nc.scalar.activation(ln_t, t1_ps[:, 0:GT], ACT.Copy).then_inc(s_lnt, 1)

            def att_out(g):
                done(eng, s_wp, g)
                done(eng, s_pv, g + 1)
                nc.scalar.activation(att_t, pv_ps[:, 0:GT], ACT.Copy).then_inc(s_att, 1)

            def x_t_out(g):
                done_apart(eng, s_t2, g + 1)
                nc.scalar.activation(
                    xt_all[:, :, bass.ds(g * GT, GT)].rearrange("p h (b t) -> p h b t", b=GROUP),
                    t2_ps.bitcast(F16).rearrange("p (h b t) -> p h b t", h=2, b=GROUP)[:, :, :, 0:T], ACT.Copy).then_inc(s_xt, 1)

            def logits_out(g):
                done_apart(eng, s_lg_mm, g + 1)
                nc.scalar.activation(logits[0:T, bass.ds(g * GROUP, GROUP), :],
                                     lg_ps[0:T, 0:GROUP * E].rearrange("p (b e) -> p b e", e=E), ACT.Copy,
                                     scale=down[0:T, 3:4]).then_inc(s_lg, 1)

            def w_high(g):
                if isinstance(g, int) and g == 0:
                    eng.wait_ge(s_gs, 2)
                for n, scale in ((0, up[:, 0:1]), (1, up[:, 2:3])):
                    c = bass.ds(g * WSTEP, WSTEP)
                    last = nc.scalar.activation(whi[:, n, c], w32[:, n, c], ACT.Copy, scale=scale)
                last.then_inc(s_whi, 1)

            def router_exp(h):
                eng.wait_ge(s_centred, h + 1)
                nc.scalar.activation(ra[0:T], logits[0:T, h * HB:(h + 1) * HB], ACT.Exp).then_inc(s_rexp, 1)

            load_table(EXP_LN_TABLE)
            pipeline(eng, [(softplus_abs, 0), (ln_t_out, 1), (softplus_log, 0), (w_high, 0, range(HG)), (att_out, 0), (x_t_out, -1), (logits_out, -1)],
                     lambda: router_exp(0))

            router_exp(1)

            def gelu(u, par, n, col):
                done_apart(eng, s_hlo, u - 1)
                for f in range(FC):
                    if f % 2 == 0:
                        done_apart(eng, s_pre[f // 2], u + 1)
                    last = nc.scalar.activation(gel[:, par, f * TILE:f * TILE + n],
                                                pre_ps[:, par, f // 2, (f % 2) * TILE:(f % 2) * TILE + n], ACT.Gelu,
                                                bias=b1[:, bass.ds(col + f, 1)], scale=down[:, 0:1])
                last.then_inc(s_gelu, 1)

            def xr_out(u, n, par):
                done(eng, s_pre[1], u - 1)
                done(eng, s_xp[par], n + 1)
                nc.scalar.activation(xr_t[:, par].rearrange("p h n -> p (h n)"),
                                     xp_ps[:, par, :].bitcast(F16)[:, 0:2 * TILE], ACT.Copy).then_inc(s_xrt[par], 1)

            def act_step(p, pair, i, c):
                (kind0, _), (kind1, n1), (kind2, n2) = pair(0), pair(1), pair(2)
                experts = [0] * 2
                if "routed" in (kind1, kind2):
                    experts = experts_of(mybir.EngineType.Activation, n1 - 1 if kind1 == "routed" else n2 - 2, 2, 4)
                for par in range(2):
                    if kind2 == "routed":
                        xr_out(p * 2 + 4 + par, n2, par)
                    kind, u = (kind1, p * 2 + 3) if par == 0 else (kind2, p * 2 + 4)
                    if kind == "shared":
                        gelu(u, 1 - par, 2 * T, (E + 1 - par) * FC)
                    if kind == "routed":
                        gelu(u, 1 - par, TILE, experts[par] * FC)

            load_table(GELU_TABLE)
            eng.wait_ge(s_routed, 2)
            run_units(eng, act_step)

        @block.vector
        def _(dve):
            eng = dve
            chain = [0]

            def link(ins):
                chain[0] += 1
                ins.then_inc(s_scale, 1)
                dve.wait_ge(s_scale, chain[0])

            eng.wait_ge(s_setup, 16 * N_SETUP)
            eng.wait_ge(s_w32, 16 * 4)
            for n, src in enumerate((w32[:, 0, :], b1[:], w32[:, 1, :], gatew[:])):
                nc.vector.tensor_reduce(mx[:, n:n + 1], src, X, ALU.max, apply_absolute_value=True).then_inc(s_mx, 1)
            eng.wait_ge(s_mxall, 1)
            link(nc.vector.scalar_tensor_tensor(mxall[:, 1:2], mxall[:, 0:1], float(D), mxall[:, 1:2], ALU.mult, ALU.add))
            link(nc.vector.tensor_scalar(mxall[:], mxall[:], LEAST, None, ALU.max))
            link(nc.vector.tensor_scalar(pw[:].bitcast(I32), mxall[:].bitcast(I32), TOPBITS, None, ALU.bitwise_and))
            link(nc.vector.reciprocal(up[:], pw[:]))
            link(nc.vector.tensor_scalar(up[:], up[:], LIFT, None, ALU.mult))
            link(nc.vector.tensor_scalar(down[:], pw[:], 1.0 / LIFT, None, ALU.mult))
            link(nc.vector.tensor_tensor(yscale[:], down[:, 1:2], down[:, 2:3], ALU.mult))
            link(nc.vector.tensor_tensor(rowb[:, 3, :], rowb[:, 3, :], rowb[:, 4, :], ALU.add))
            nc.vector.tensor_scalar(gsplit[:, 0], gatew[:], up[:, 3:4], None, ALU.mult).then_inc(s_gs, 1)
            eng.wait_ge(s_gs, 1)
            nc.vector.scalar_tensor_tensor(gsplit[:, 1], gatew[:], up[:, 3:4], gsplit[:, 0], ALU.mult, ALU.subtract).then_inc(s_gs, 1)

            def rows(g):
                return h_all[0:T, bass.ds(g * GROUP, GROUP), :]

            def stats(g, st, s_src, s_a):
                done_apart(eng, s_src, g + 1)
                for b in range(GROUP):
                    last = nc.vector.bn_stats(st[0:T, b, :], rows(g)[:, b, :])
                last.then_inc(s_a, 1)

            def moments(g, st, mv, s_a, s_before, s_done):
                done_apart(eng, s_before, g)
                done_apart(eng, s_a, g + 1)
                for b in range(GROUP):
                    last = nc.vector.bn_aggr(mv[0:T, b, :], st[0:T, b, :])
                last.then_inc(s_done, 1)

            def stats1(g):
                done_apart(eng, s_st1, g)
                stats(g, st1, s_h, s_st1a)

            def stats2(g):
                done_apart(eng, s_st2, g)
                stats(g, st2, s_h2, s_st2a)

            def moments1(g):
                moments(g, st1, mv1, s_st1a, s_ln, s_st1)

            def moments2(g):
                moments(g, st2, mv2, s_st2a, s_xn, s_st2)

            def h_out(g):
                done(eng, s_h_mm, g + 1)
                nc.vector.tensor_tensor(rows(g), h_ps[0:T, 0:GROUP * D].rearrange("p (b n) -> p b n", n=D),
                                        rowb[0:T, 0:1, :].to_broadcast([T, GROUP, D]), ALU.add).then_inc(s_h, 1)

            def ln_out(g):
                done(eng, s_t1, g)
                done(eng, s_rs1, g + 1)
                for b in range(GROUP):
                    last = nc.vector.tensor_scalar(ln[0:T, b, :], h_all[0:T, bass.ds(g * GROUP + b, 1), :].rearrange("p b n -> p (b n)"),
                                                   mv1[0:T, b, 0:1], rs1[0:T, b:b + 1], ALU.subtract, ALU.mult)
                last.then_inc(s_ln, 1)

            def rope_parts(g):
                done(eng, s_rope, g)
                done(eng, s_qk, g + 1)
                for n, src in enumerate((q_ps, qs_ps, k_ps, ks_ps)):
                    last = nc.vector.scalar_tensor_tensor(
                        rparts[:, n].rearrange("p (b t) -> p b t", t=T), src[:, 0:GT].rearrange("p (b t) -> p b t", t=T),
                        colb[:, n:n + 1], rope[:, n:n + 1, :].to_broadcast([P, GROUP, T]), ALU.add, ALU.mult)
                last.then_inc(s_rp, 1)

            def v_out(g):
                done(eng, s_pv, g)
                done(eng, s_v_mm, g + 1)
                nc.vector.tensor_tensor(v_tok[0:T], v_ps[0:T, 0:GROUP * D].rearrange("p (b n) -> p b n", n=D),
                                        rowb[0:T, 1:2, :].to_broadcast([T, GROUP, D]), ALU.add).then_inc(s_v, 1)

            def weights(g):
                done(eng, s_pv, g)
                done(eng, s_lnp, g + 1)
                nc.vector.scalar_tensor_tensor(wei[0:T], s_ps[0:T, 0:GT], 0.0, sp[0:T], ALU.max, ALU.add).then_inc(s_wei, 1)

            def h2_out(g):
                done(eng, s_hb, g + 1)
                done(eng, s_wp, g + 1)
                nc.vector.tensor_tensor(rows(g), wp_ps[0:T, 0:GROUP * D].rearrange("p (b n) -> p b n", n=D), rows(g),
                                        ALU.add).then_inc(s_h2, 1)

            def x_out(g):
                done(eng, s_xlo, g)
                done(eng, s_rs2, g + 1)
                for b in range(GROUP):
                    last = nc.vector.tensor_scalar(xn[0:T, b, :], h_all[0:T, bass.ds(g * GROUP + b, 1), :].rearrange("p b n -> p (b n)"),
                                                   mv2[0:T, b, 0:1], rs2[0:T, b:b + 1], ALU.subtract, ALU.mult)
                last.then_inc(s_xn, 1)
                done(eng, s_t2, g)
                done(eng, s_xtok, g, 16)
                done(eng, s_xn, g + 1)
                nc.vector.tensor_copy(xsplit[0:T, :, 0, :], xn[0:T]).then_inc(s_xhi, 1)
                done(eng, s_xhi, g + 1)
                nc.vector.tensor_tensor(xsplit[0:T, :, 1, :], xn[0:T], xsplit[0:T, :, 0, :], ALU.subtract).then_inc(s_xlo, 1)

            def w_low(g):
                done(eng, s_whi, g + 1)
                for n, scale in ((0, up[:, 0:1]), (1, up[:, 2:3])):
                    c = bass.ds(g * WSTEP, WSTEP)
                    last = nc.vector.scalar_tensor_tensor(wlo[:, n, c], w32[:, n, c], scale, whi[:, n, c], ALU.mult, ALU.subtract)
                last.then_inc(s_wlo, 1)

            n_r = [0]

            def link_r(ins):
                n_r[0] += 1
                ins.then_inc(s_r, 1)
                dve.wait_ge(s_r, n_r[0])

            def over_e(v):
                return v.rearrange("p (b e) -> p b e", e=1).to_broadcast([T, HB, E])

            def over_b(v):
                return v.rearrange("p (b e) -> p b e", b=1).to_broadcast([T, HB, E])

            def routing(h):
                L, A, C = logits[0:T, h * HB:(h + 1) * HB], ra[0:T], rc[0:T]
                gate_values = gatev[0:T, :, h * HB:(h + 1) * HB]
                v = [rvec[0:T, n, :] for n in range(4)]
                eng.wait_ge(s_lg, HG * (h + 1))
                eng.wait_ge(s_wlo, HG)
                link_r(nc.vector.tensor_tensor(L, L, over_b(gateb[0:T]), ALU.add))
                link_r(nc.vector.tensor_reduce(v[0], L, X, ALU.max))
                nc.vector.tensor_tensor(L, L, over_e(v[0]), ALU.subtract).then_inc(s_centred, 1)
                eng.wait_ge(s_rexp, h + 1)
                link_r(nc.vector.tensor_reduce(v[1], A, X, ALU.add))
                link_r(nc.vector.reciprocal(v[2], v[1]))
                link_r(nc.vector.tensor_tensor(A, A, over_e(v[2]), ALU.mult))
                src = A
                for k in range(TOP):
                    link_r(nc.vector.tensor_reduce(gate_values[:, k], src, X, ALU.max))
                    link_r(nc.vector.tensor_tensor(C, src, over_e(gate_values[:, k]), ALU.is_equal))
                    link_r(nc.vector.tensor_tensor(C, C, over_b(prefer_low[0:T]), ALU.mult))
                    link_r(nc.vector.tensor_reduce(v[3], C, X, ALU.max))
                    link_r(nc.vector.tensor_tensor(oh[0:T, k], over_b(prefer_low[0:T]), over_e(v[3]), ALU.is_equal))
                    if k == 0:
                        link_r(nc.vector.scalar_tensor_tensor(C, oh[0:T, 0], -2.0, A, ALU.mult, ALU.add))
                        src = C
                nc.vector.tensor_tensor(chosen[0:T].rearrange("p (b e) -> p b e", e=E), oh[0:T, 0], oh[0:T, 1], ALU.add).then_inc(s_chosen, 1)
                eng.wait_ge(s_rank, h + 1)
                rank = rank_ps[0:T, 0:HB * E].rearrange("p (b e) -> p b e", e=E)
                total = rank_ps[0:T, HB * E:2 * HB * E].rearrange("p (b e) -> p b e", e=E)
                for e in range(E):
                    last = nc.vector.tensor_tensor_scan(run[0:T, e, :], ones64[0:T, 0:HB], total[:, :, e], 0.0, ALU.mult, ALU.add)
                link_r(last)
                link_r(nc.vector.tensor_tensor(A, run[0:T].rearrange("p e b -> p b e"), total, ALU.subtract))
                nc.vector.tensor_tensor(A, A, rank, ALU.add).then_inc(s_rank_read, 1)
                eng.wait_ge(s_rank_read, h + 1)
                full = cmp[0:T, 0:E * MAXT].rearrange("p (e n) -> p e n", e=E)
                link_r(nc.vector.tensor_copy(te[0:T, 0], run[0:T, :, HB - 1]))
                link_r(nc.vector.tensor_tensor(full, te[0:T, 0].rearrange("p (e n) -> p e n", n=1).to_broadcast([T, E, MAXT]),
                                               tile_steps[0:T].rearrange("p (e n) -> p e n", e=1).to_broadcast([T, E, MAXT]), ALU.is_gt))
                link_r(nc.vector.tensor_reduce(te[0:T, 1], full, X, ALU.add))
                link_r(nc.vector.tensor_tensor_scan(te[0:T, 2], ones64[0:T, 0:E], te[0:T, 1], 0.0, ALU.mult, ALU.add))
                link_r(nc.vector.tensor_tensor(te[0:T, 3], te[0:T, 2], te[0:T, 1], ALU.subtract))
                link_r(nc.vector.tensor_scalar(te[0:T, 3], te[0:T, 3], float(TILE), float(h * HTILES * TILE), ALU.mult, ALU.add))
                passed = cmp[0:1, 0:HTILES * (E - 1)].rearrange("p (n e) -> p n e", e=E - 1)
                link_r(nc.vector.tensor_tensor(passed, tile_ids[0:1].rearrange("p (n e) -> p n e", e=1).to_broadcast([1, HTILES, E - 1]),
                                               te[0:1, 2, 0:E - 1].rearrange("p (n e) -> p n e", n=1).to_broadcast([1, HTILES, E - 1]), ALU.is_ge))
                link_r(nc.vector.tensor_reduce(tile_exf[:], passed, X, ALU.add))
                by_pair = tile_exf[:].rearrange("p (n k) -> p n k", k=2)
                for lo, hi, row, k in ((0, 2, 2, 0), (2, 3, 1, 1), (3, 4, 0, 0)):
                    row += h * HTILES // 2
                    link_r(nc.vector.tensor_copy(tile_ex[:, row:row + HTILES // 2, lo:hi], by_pair[:, :, k:k + hi - lo]))
                link_r(nc.vector.tensor_tensor(A, A, over_b(te[0:T, 3]), ALU.add))
                for k in range(TOP):
                    link_r(nc.vector.tensor_tensor(C, oh[0:T, k], A, ALU.mult))
                    link_r(nc.vector.tensor_reduce(posf[0:T, :, k], C, X, ALU.add))
                nc.vector.tensor_copy(pos[0:T, h * HB:(h + 1) * HB], posf[0:T]).then_inc(s_routed, 1)
                eng.wait_ge(s_routed, h + 1)

            link_r(nc.vector.memset(tile_ex[:], 0))
            pipeline(eng, [(h2_out, -1), (h_out, 2), (stats2, -1), (stats1, 2), (moments2, -1), (moments1, 2),
                           (weights, 0), (x_out, -1), (rope_parts, 1), (ln_out, 2), (v_out, 1),
                           (w_low, 0, range(HG))], lambda: routing(0))
            routing(1)

            def split(u, par, n):
                g = gel[:, par].rearrange("p (f n) -> p f n", f=FC)[:, :, 0:n]
                done(eng, s_y_mm, u - 1)
                done(eng, s_gelu, u + 1)
                nc.vector.tensor_scalar(hhi[:, par, :, 0:n], g, up[:, 1:2], None, ALU.mult).then_inc(s_hhi, 1)
                done(eng, s_hhi, u + 1)
                nc.vector.scalar_tensor_tensor(hlo[:, par, :, 0:n], g, up[:, 1:2], hhi[:, par, :, 0:n], ALU.mult, ALU.subtract).then_inc(s_hlo, 1)

            def add_shared(u, j):
                done(eng, s_y_mm, u + 1)
                hj = h_all[0:T, bass.ds(j * 2, 2), :]
                nc.vector.scalar_tensor_tensor(hj, y_ps[0:T, :, 0:D], yscale[0:T], hj, ALU.mult, ALU.add).then_inc(s_ysh, 1)

            def tile_output(u, n, par, e):
                done(eng, s_yst[par], n, 16)
                done(eng, s_y_mm, u + 1)
                nc.vector.scalar_tensor_tensor(
                    y_out[:, par], y_ps[:, par, 0:SUB * D].rearrange("p (s n) -> p s n", n=D), yscale[:],
                    b2[:, bass.ds(e, 1), :].to_broadcast([P, SUB, D]), ALU.mult, ALU.add).then_inc(s_yr[par], 1)

            def combine(n, par):
                g = n * 2 + par
                done(eng, s_gat[par], n + 1, 16 * GROUP * TOP)
                done(eng, s_ysh, (g + 1) * 2)
                for k in range(TOP):
                    for b in range(GROUP):
                        row = h_all[0:T, bass.ds(g * GROUP + b, 1), :].rearrange("p b n -> p (b n)")
                        last = nc.vector.scalar_tensor_tensor(
                            row, gat[0:T, par, b, k, :], gatev[0:T, k, bass.ds(g * GROUP + b, 1)], row, ALU.mult, ALU.add)
                    if k == 0:
                        last.then_inc(s_half, 1)
                        done(eng, s_half, g + 1)
                last.then_inc(s_comb[par], 1)

            starts_b = SJA + NTILES // 2

            def dve_step(p, pair, i, c):
                (kind0, n0), (kind1, n1) = pair(0), pair(1)
                if kind0 == "routed":
                    experts = experts_of(mybir.EngineType.DVE, n0, 0, 2)
                for par in range(2):
                    if kind0 == "shared" and par == 1:
                        add_shared(p * 2 + 1, n0)
                    if kind1 is not None:
                        split(p * 2 + 2 + par, par, TILE if kind1 == "routed" else 2 * T)
                    if kind0 == "routed":
                        tile_output(p * 2 + par, n0, par, experts[par])
                number = c - starts_b
                if number == 0:
                    combine(0, 0)
                elif number > 0 and number % 2:
                    g = (number + 1) // 2
                    combine(i + g // 2, g % 2)

            run_units(eng, dve_step, unroll=4)
            for g in range((SJ - SJA) // 2 + 1, NG):
                combine(g // 2, g % 2)


def kernel(**inputs):
    import numpy as np
    import concourse.bacc as bacc
    from concourse.bass_utils import run_bass_kernel_spmd
    import ml_dtypes

    def arr(name):
        return np.asarray(inputs[name])

    def cols(v):
        return v.reshape(-1, 1)

    def on_all(v):
        return np.broadcast_to(v, (P,) + v.shape)

    swap = np.arange(D).reshape(-1, 2)[:, ::-1].reshape(-1)
    where = np.arange(T - 1, -1, -1, dtype=np.float32)
    angle = (where[None, :] * np.arange(D // 2, dtype=np.float32)[:, None]).astype(np.float64)
    cos = np.repeat(np.cos(angle), 2, axis=0)
    sin = np.repeat(np.sin(angle), 2, axis=0) * np.tile([-1.0, 1.0], D // 2)[:, None]
    q_scale = float(D) ** -0.5
    rope = np.stack([cos * q_scale, sin * q_scale, cos, sin], axis=1).astype(np.float32)
    eye = np.eye(P)
    masked = np.where(np.arange(P)[None, :] < np.arange(P)[:, None], -1e30, 0.0)
    earlier = (np.arange(P)[:, None] < np.arange(P)[None, :]).astype(np.float32)
    counts = np.concatenate([np.arange(MAXT) * TILE, np.arange(HTILES), E - np.arange(E)]).astype(np.float32)

    wq, wk, bq, bk = arr("L0_attn_Wq"), arr("L0_attn_Wk"), arr("L0_attn_bq"), arr("L0_attn_bk")
    arrays = {
        "x": arr("x").reshape(B * T, CTX, D).transpose(2, 1, 0),
        "wt": arr("L0_tok_weight").reshape(D, CTX, D).transpose(2, 1, 0),
        "wmat": np.stack([wq, wq[:, swap], wk, wk[:, swap], arr("L0_attn_Wv"), arr("L0_attn_Wp")], axis=1),
        "rope": rope,
        "colb": np.concatenate([cols(bq), cols(bq[swap]), cols(bk), cols(bk[swap])], axis=1),
        "rowb": on_all(np.stack([arr("L0_tok_bias"), arr("L0_attn_bv"), arr("L0_attn_bp"),
                                 arr("L0_ffn_sb2")[0], arr("L0_ffn_sb2")[1]])),
        "gateb": on_all(arr("L0_ffn_gate_b")),
        "gatew": arr("L0_ffn_gate_w").T,
        "rb1": arr("L0_ffn_rb1").reshape(E * FC, P).T,
        "sb1": arr("L0_ffn_sb1").reshape(NS * FC, P).T,
        "rb2": on_all(arr("L0_ffn_rb2")),
        "rw1": arr("L0_ffn_rw1").transpose(2, 0, 1).reshape(D, E * F),
        "sw1": arr("L0_ffn_sw1").transpose(2, 0, 1).reshape(D, NS * F),
        "rw2": arr("L0_ffn_rw2").reshape(E, D, FC, P).transpose(3, 0, 2, 1).reshape(P, E * F),
        "sw2": arr("L0_ffn_sw2").reshape(NS, D, FC, P).transpose(3, 0, 2, 1).reshape(P, NS * F),
        "ident": eye.astype(np.float32),
        "identh": eye.astype(np.float16),
        "maskl": np.stack([eye, masked], axis=1).astype(ml_dtypes.bfloat16),
        "tri": np.stack([earlier, np.ones((P, P), np.float32)], axis=1).astype(ml_dtypes.bfloat16),
        "counts": on_all(counts),
    }
    arrays = {k: np.ascontiguousarray(v) for k, v in arrays.items()}
    nc = bacc.Bacc("TRN2", target_bir_lowering=False, num_devices=1)
    d = {k: nc.dram_tensor(f"in_{k}", v.shape, mybir.dt.from_np(v.dtype), kind="ExternalInput").ap() for k, v in arrays.items()}
    out = nc.dram_tensor("out", [B, T, D], F32, kind="ExternalOutput").ap()
    build(nc, d, out)
    r = run_bass_kernel_spmd(nc, [{f"in_{k}": v for k, v in arrays.items()}], core_ids=[0])
    return r.results[0]["out"]
```

```python
from contextlib import ExitStack

import concourse.bass as bass
from concourse import mybir

F32 = mybir.dt.float32
F16 = mybir.dt.float16
BF16 = mybir.dt.bfloat16
I32 = mybir.dt.int32
ALU = mybir.AluOpType
ACT = mybir.ActivationFunctionType
X = mybir.AxisListType.X
ABSMAX = bass.bass_isa.ReduceOp.max

P = 128
B = 64
T = 125
CTX = 3
D = 128
E = 8
NS = 2
NE = E + NS
F = 512
FC = F // P
TOP = 2
EPS = 1e-5
GROUP = 4
NG = B // GROUP
GT = GROUP * T
TILE = 256
SUB = TILE // P
PART_GROUPS = (5, 11)
PART_B = [n * GROUP for n in PART_GROUPS]
PART_TILES = [(n * T * TOP + E * (TILE - 1)) // TILE for n in PART_B]
PART_TILES = [n + n % 2 for n in PART_TILES]
MAXB = max(PART_B)
PTILES = max(PART_TILES)
NTILES = sum(PART_TILES)
SLOTS = NTILES * TILE
MAXT = -(-MAXB * T // TILE)
SJ = B // 2
SJA = 10
TURN_GROUPS = 2
WCOLS = NE * F
WGROUPS = PART_GROUPS[0] + 1
WSTEP = -(-WCOLS // (WGROUPS * 16)) * 16
TOPBITS = 0x7F800000
BPARTS = 3
CLEAR = 2 * TILE
ZROWS = 2
EXP_LN_TABLE = 6
GELU_TABLE = 10
LIFT = 2.0 ** 14
LEAST = 2.0 ** -40


def build(nc, d, out):
    x_tok = nc.dram_tensor("x_tok", [B * T, 2 * D], F16).ap()
    x_slots = [nc.dram_tensor(f"x_slots{h}", [PART_TILES[h] * TILE, 2 * D], F16).ap() for h in range(2)]
    y_slots = [nc.dram_tensor(f"y_slots{h}", [PART_TILES[h] * TILE, D], F32).ap() for h in range(2)]

    with ExitStack() as ctx:
        def sb(name, shape, dt):
            return ctx.enter_context(nc.sbuf_tensor(name, shape, dt))

        def psum(name, shape, dt):
            return ctx.enter_context(nc.psum_tensor(name, shape, dt))

        def sem(name):
            return ctx.enter_context(nc.semaphore(name))

        pre_ps = psum("pre_ps", [P, 2, 2, 512], F32)
        xp_ps = psum("xp_ps", [P, 2, 512], F32)
        y_ps = psum("y_ps", [P, 2, 512], F32)
        q_ps, qs_ps = pre_ps[:, 0, 0, :], pre_ps[:, 0, 1, :]
        k_ps, ks_ps = pre_ps[:, 1, 0, :], pre_ps[:, 1, 1, :]
        v_ps, wp_ps = q_ps, qs_ps
        s_ps, t1_ps = xp_ps[:, 0, :], xp_ps[:, 1, :]
        lg_ps = t1_ps
        t2_ps, h_ps = y_ps[:, 0, :], y_ps[:, 1, :]
        pv_ps = t2_ps
        def rank_banks(h):
            n = PART_B[h] * E
            return (t2_ps[0:T, 0:n], t2_ps[0:T, n:2 * n] if h == 0 else h_ps[0:T, 0:n])


        wt = sb("wt", [P, CTX, D], F32)
        wmat = sb("wmat", [P, 6, D], F32)
        rope = sb("rope", [P, 4, T], F32)
        colb = sb("colb", [P, 4], F32)
        rowb = sb("rowb", [P, 5, D], F32)
        bias = sb("bias", [BPARTS, 3, D], BF16)
        onesh = sb("onesh", [BPARTS, P], BF16)
        gateb = sb("gateb", [P, E], F32)
        ident = sb("ident", [P, P], F32)
        identh = sb("identh", [P, P], F16)
        maskl = sb("maskl", [P, 2, P], BF16)
        tri = sb("tri", [P, 2, P], BF16)
        counts_const = sb("counts_const", [P, MAXT + PTILES + E], F32)
        tile_steps = counts_const[:, 0:MAXT]
        tile_ids = counts_const[:, MAXT:MAXT + PTILES]
        prefer_low = counts_const[:, MAXT + PTILES:]
        gatew = sb("gatew", [P, E], F32)
        b1 = sb("b1", [P, NE * FC], F32)
        b2 = sb("b2", [P, E, D], F32)
        epsc = sb("epsc", [P, 2, GROUP], F32)
        ones64 = sb("ones64", [P, B], F32)
        zeros = sb("zeros", [P, ZROWS * 2 * D], F16)
        w32 = sb("w32", [P, 2, WCOLS], F32)
        whi = sb("whi", [P, 2, WCOLS], F16)
        wlo = sb("wlo", [P, 2, WCOLS], F16)
        gsplit = sb("gsplit", [P, 2, E], F16)
        mx = sb("mx", [P, 4], F32)
        mxall = sb("mxall", [P, 4], F32)
        pw = sb("pw", [P, 4], F32)
        up = sb("up", [P, 4], F32)
        down = sb("down", [P, 4], F32)
        yscale = sb("yscale", [P, 1], F32)

        flow = sb("flow", [P, 16 * 512], F32)
        taken = [0]

        def carve(n):
            taken[0] += n
            assert taken[0] <= 16 * 512
            return flow[:, taken[0] - n:taken[0]]

        x_in = carve(CTX * GT).rearrange("p (c n) -> p c n", c=CTX)
        h_all = sb("h_all", [P, B, D], F32)
        st1 = sb("st1", [P, GROUP, 6], F32)
        mv1 = sb("mv1", [P, GROUP, 2], F32)
        rs1 = sb("rs1", [P, GROUP], F32)
        ve1 = sb("ve1", [P, GROUP], F32)
        ln = carve(GROUP * D).rearrange("p (b n) -> p b n", b=GROUP)
        ln_t = carve(GT)
        rparts = carve(4 * GT).rearrange("p (a n) -> p a n", a=4)
        q_t = carve(GT)
        bias_parts = rparts.rearrange("p a n -> p (a n)")[0:BPARTS, 0:12 * D].rearrange("p (k r n) -> p k r n", k=4, r=3)
        part16 = q_t[0:BPARTS, 0:3 * D // 2].bitcast(BF16).rearrange("p (r n) -> p r n", r=3)
        k_t = carve(GT)
        v_tok = carve(GROUP * D).rearrange("p (b n) -> p b n", b=GROUP)
        sp = carve(GT)
        wei = carve(GT)
        att_t = carve(GT)
        st2 = sb("st2", [P, GROUP, 6], F32)
        mv2 = sb("mv2", [P, GROUP, 2], F32)
        rs2 = sb("rs2", [P, GROUP], F32)
        ve2 = sb("ve2", [P, GROUP], F32)
        xn = carve(GROUP * D).rearrange("p (b n) -> p b n", b=GROUP)
        xsplit = sb("xsplit", [P, GROUP, 2, D], F16)
        xt_all = sb("xt_all", [P, 2, B * T], F16)
        logits = sb("logits", [P, B, E], F32)

        chosen = sb("chosen", [P, MAXB * E], BF16)
        rvec = sb("rvec", [P, 4, MAXB], F32)
        gatev = sb("gatev", [P, TOP, B], F32)
        te = sb("te", [P, 4, E], F32)
        posf = sb("posf", [P, MAXB, TOP], F32)
        pos = sb("pos", [P, B, TOP], I32)
        tile_exf = sb("tile_exf", [1, PTILES], F32)
        tile_ex = sb("tile_ex", [1, NTILES // 2 + 2, 4], I32)

        w32f = w32[:, :, :].rearrange("p a n -> p (a n)")
        gel = w32f[:, 0:2 * FC * TILE].rearrange("p (b n) -> p b n", b=2)
        gel4 = gel.rearrange("p b (f n) -> p b f n", f=FC)
        o = 2 * FC * TILE
        rows_a = w32f[:, o:o + PART_B[0] * D].bitcast(F16).rearrange("p (b n) -> p b n", n=2 * D)
        gat = w32f[:, o:o + 2 * GROUP * TOP * D].rearrange("p (b g k n) -> p b g k n", b=2, g=GROUP, k=TOP)
        o += max(PART_B[0] * D, 2 * GROUP * TOP * D)
        cmp = w32f[:, o:o + 512]
        o += 512
        ra_all, rc_all, run_all = (w32f[:, o + n * MAXB * E:o + (n + 1) * MAXB * E] for n in range(3))
        o += 3 * MAXB * E
        oh_all = w32f[:, o:o + TOP * MAXB * E].rearrange("p (k n) -> p k n", k=TOP)
        o += TOP * MAXB * E
        hhi, hlo = (w32f[:, o + n * FC * TILE:o + (n + 1) * FC * TILE].bitcast(F16)
                    .rearrange("p (b f n) -> p b f n", b=2, f=FC) for n in range(2))
        o += 2 * FC * TILE
        assert o <= 2 * WCOLS
        xr_t = sb("xr_t", [P, 2, 2, TILE], F16)
        rows_b = flow[:, 0:PART_B[1] * D].bitcast(F16).rearrange("p (b n) -> p b n", n=2 * D)
        o = PART_B[1] * D
        xr_in = flow[:, o:o + 2 * SUB * D].bitcast(F16).rearrange("p (b s n) -> p b s n", b=2, s=SUB)
        o += 2 * SUB * D
        y_out = flow[:, o:o + 2 * SUB * D].rearrange("p (b s n) -> p b s n", b=2, s=SUB)
        srow = sb("srow", [P, 2, 2 * D], F16)
        sidx = sb("sidx", [P, 2, TOP], I32)
        gidx = sb("gidx", [P, 2, GROUP, TOP], I32)
        s_first, s_setup = sem("first_setup_loaded"), sem("setup_loaded")
        s_bias_chain, s_bias = sem("bias_chain"), sem("bias_parts_done")
        s_w32 = [sem(f"w{n + 1}_loaded") for n in range(2)]
        s_const = sem("consts_set")
        s_zero = [sem(f"part{h}_zeroed") for h in range(2)]
        s_mx = sem("maxima_taken")
        s_mxall = sem("maxima_joined")
        s_scale = sem("scales_chain")
        s_gs = sem("gate_split")
        s_x = sem("x_loaded")
        s_h_mm = sem("h_products")
        s_h = sem("h_stored")
        s_st1a, s_st1, s_ve1, s_rs1, s_ln = (sem(n) for n in ("ln1_stats", "ln1_moments", "ln1_var_eps", "ln1_rstd", "ln1_done"))
        s_t1, s_lnt = sem("ln1_transposed"), sem("ln1_t_stored")
        s_qk, s_rp, s_rope = sem("qk_products"), sem("rope_parts"), sem("rope_done")
        s_v_mm, s_v = sem("v_products"), sem("v_stored")
        s_s, s_abs, s_exp, s_lnp, s_wei = (sem(n) for n in ("scores", "score_abs", "score_exp", "score_log", "weights_done"))
        s_pv, s_att, s_wp, s_h2 = (sem(n) for n in ("pv_products", "att_stored", "wp_products", "h2_done"))
        s_st2a, s_st2, s_ve2, s_rs2, s_xn = (sem(n) for n in ("ln2_stats", "ln2_moments", "ln2_var_eps", "ln2_rstd", "ln2_done"))
        s_xhi, s_xlo, s_xtok, s_hb2 = (sem(n) for n in ("x_high", "x_low", "x_tok_stored", "h2_plus_b2"))
        s_t2, s_xt, s_lg_mm, s_lg = (sem(n) for n in ("x_transposed", "x_t_stored", "gate_products", "logits_stored"))
        s_whi, s_wlo = sem("w_high"), sem("w_low")
        s_r = sem("routing_chain")
        s_centred, s_rexp = sem("logits_centred"), sem("router_exp")
        s_rank, s_rank_read = sem("rank_products"), sem("ranks_read")
        s_routed, s_tiles = sem("slots_known"), sem("tile_experts_known")
        s_chosen = sem("experts_chosen")
        s_rows = [sem(f"part{h}_rows_loaded") for h in range(2)]
        s_stage, s_gidx = sem("batch_staged"), sem("gather_indices_staged")
        s_scat = [sem(f"scattered{p}") for p in range(2)]
        s_xr = [sem(f"tile_loaded{p}") for p in range(2)]
        s_xp = [sem(f"tile_transposed{p}") for p in range(2)]
        s_xrt = [sem(f"tile_t_stored{p}") for p in range(2)]
        s_pre = [sem(f"pre_half{p}") for p in range(2)]
        s_gelu, s_hhi, s_hlo = sem("gelu_done"), sem("hidden_high"), sem("hidden_low")
        s_last_high = sem("shared_last_high")
        s_y_mm, s_ysh = sem("unit_outputs"), sem("shared_added")
        s_yr = [sem(f"tile_output{p}") for p in range(2)]
        s_yst = [sem(f"tile_stored{p}") for p in range(2)]
        s_gat = [sem(f"gathered{p}") for p in range(2)]
        s_quarter, s_out = sem("quarters_added"), sem("out_stored")
        s_comb = [sem(f"experts_added{p}") for p in range(2)]

        block = ctx.enter_context(nc.Block())

        def done(eng, s, n, step=1):
            if isinstance(n, int):
                if n > 0:
                    eng.wait_ge(s, n * step)
            else:
                eng.wait_ge(s, n * step if step != 1 else n)

        def done_apart(eng, s, n, step=1):
            if isinstance(n, int):
                done(eng, s, n, step)
            else:
                value = eng.to_reg(n * step if step != 1 else n)
                eng.wait_ge(s_const, 1)
                eng.wait_ge(s, value)

        def split_columns(g):
            return bass.ds(g * WSTEP, min(WSTEP, WCOLS - g * WSTEP) if isinstance(g, int) else WSTEP)

        def upto(n):
            return min(n, NG) if isinstance(n, int) else n

        def pipeline(eng, stages, midway):
            stages = [(s[0], s[1], s[2] if len(s) > 2 else range(NG)) for s in stages]
            first = min(r.start - lag for _, lag, r in stages)
            last = max(r.stop - 1 - lag for _, lag, r in stages)
            lo = max(-lag for _, lag, _ in stages) + 1
            hi = min(NG - lag for _, lag, _ in stages)
            mid = PART_GROUPS[0] + 1

            def step(i, where):
                for stage, lag, r in stages:
                    if where + lag in r:
                        stage(i + lag)

            for i in range(first, lo):
                step(i, i)
            with eng.Fori(lo, mid - 1) as i:
                step(i, lo)
            step(mid - 1, mid - 1)
            midway()
            with eng.Fori(mid, hi) as i:
                step(i, mid)
            for i in range(hi, last + 1):
                step(i, i)

        N_FIRST, N_SETUP = 3, 12

        segments = [("shared", SJA, 0), ("routed", NTILES // 2, 0), ("shared", SJ - SJA, SJA)]

        def run_units(eng, step, unroll=1, cut=None):
            starts = [sum(pairs for _, pairs, _ in segments[:m]) for m in range(len(segments))]
            total = starts[-1] + segments[-1][1]

            def at(p):
                def pair(k):
                    for (kind, pairs, first), start in zip(segments, starts):
                        if start <= p + k < start + pairs:
                            return kind, p + k - start + first
                    return None, 0
                return pair

            def step_in_loop(kind, i, c, local, length):
                step(i * length + c, lambda k: (kind, i * length + (local + k)), i, c)

            p = -2
            for (kind, pairs, first), start in zip(segments, starts):
                while p < start + 2:
                    step(p, at(p), 0, p)
                    p += 1
                loops = [(start + pairs - 2, unroll)]
                if cut is not None and kind == "routed":
                    loops = [(cut, unroll), (start + pairs - 2, 4 * TURN_GROUPS)]
                for end, length in loops:
                    turns = (end - p) // length
                    if turns > 0:
                        with eng.Fori(0, turns) as i:
                            for c in range(p, p + length):
                                step_in_loop(kind, i, c, c - start + first, length)
                        p += turns * length
            while p < total:
                step(p, at(p), 0, p)
                p += 1

        def experts_of(engine, n, lo, hi):
            _, values = nc.values_load_multi_w_load_instructions(
                tile_ex[0:1, bass.ds(n + 2, 1), lo:hi].rearrange("p n k -> p (n k)"), engines=[engine],
                min_val=0, max_val=E - 1,
                skip_runtime_bounds_check_because="a count of passed boundaries between E experts is at most E - 1")
            return values

        @block.sync
        def _(sp_eng):
            eng = sp_eng
            first_loads = [(wt[:], d["wt"]), (rowb[:], d["rowb"]), (ident[:], d["ident"])]
            loads = [(wmat[:], d["wmat"]), (rope[:], d["rope"]), (colb[:], d["colb"]), (maskl[:], d["maskl"]),
                     (identh[:], d["identh"]), (gateb[:], d["gateb"]), (gatew[:], d["gatew"]), (tri[:], d["tri"]),
                     (counts_const[:], d["counts"]), (b1[:, 0:E * FC], d["rb1"]), (b1[:, E * FC:], d["sb1"]),
                     (b2[:], d["rb2"])]
            clears = [n * TILE // CLEAR for n in PART_TILES]
            assert sum(clears) * CLEAR == SLOTS and CLEAR % (P * ZROWS) == 0
            assert len(first_loads) == N_FIRST and len(loads) == N_SETUP
            x_d = d["x"]

            def load_x(g):
                done(eng, s_h_mm, g)
                eng.dma_start(x_in, x_d[:, :, bass.ds(g * GT, GT)]).then_inc(s_x, 16)

            def store_x_tok(g):
                done_apart(eng, s_xlo, g + 1)
                eng.dma_start(x_tok[bass.ds(g * GT, GT), :].rearrange("(b t) n -> t b n", t=T),
                              xsplit[0:T].rearrange("p b h n -> p b (h n)")).then_inc(s_xtok, 16)

            for dst, src in first_loads:
                eng.dma_start(dst, src).then_inc(s_first, 16)
            load_x(0)
            for dst, src in loads:
                eng.dma_start(dst, src).then_inc(s_setup, 16)
            def load_weights(n):
                eng.dma_start(w32[:, n, 0:E * F], d[f"rw{n + 1}"]).then_inc(s_w32[n], 16)
                eng.dma_start(w32[:, n, E * F:], d[f"sw{n + 1}"]).then_inc(s_w32[n], 16)

            def clear(h, n):
                eng.dma_start(x_slots[h][bass.ds(n * CLEAR, CLEAR), :].rearrange("(p a r) n -> p a (r n)", p=P, r=ZROWS),
                              zeros[:].rearrange("p (a n) -> p a n", a=1).to_broadcast([P, CLEAR // P // ZROWS, ZROWS * 2 * D])
                              ).then_inc(s_zero[h], 16)

            load_weights(0)
            load_x(1)
            load_weights(1)
            eng.wait_ge(s_const, 3)
            for g in range(2, 4):
                load_x(g)
            with eng.Fori(4, PART_GROUPS[0] + 4) as g:
                load_x(g)
                store_x_tok(g - 4)
                for n in range(2):
                    clear(0, (g - 4) * 2 + n)

            def load_rows(dst, h):
                eng.wait_ge(s_xtok, 16 * sum(PART_GROUPS[:h + 1]))
                b = sum(PART_B[:h])
                eng.dma_start(dst[0:T], x_tok[b * T:(b + PART_B[h]) * T, :].rearrange("(b t) n -> t b n", t=T)
                              ).then_inc(s_rows[h], 16)
            load_x(PART_GROUPS[0] + 4)
            eng.wait_ge(s_wlo, WGROUPS)
            load_rows(rows_a, 0)
            for n in range(PART_GROUPS[0] * 2, clears[0]):
                clear(0, n)
            store_x_tok(PART_GROUPS[0])
            turns, each = NG - PART_GROUPS[0] - 5, 4
            with eng.Fori(0, turns) as n:
                load_x(n + (PART_GROUPS[0] + 5))
                store_x_tok(n + (PART_GROUPS[0] + 1))
                for c in range(each):
                    clear(1, n * each + c)
            for n in range(turns * each, clears[1]):
                clear(1, n)
            for g in range(NG - 4, NG):
                store_x_tok(g)
            load_rows(rows_b, 1)

            def wait_scattered(h):
                for par in range(2):
                    eng.wait_ge(s_scat[par], 16 * TOP * sum(PART_B[:h + 1]) // 2)

            first_tile = (0, PART_TILES[0])

            def load_tile(n, par, part):
                done_apart(eng, s_xp[par], n)
                eng.dma_start(xr_in[:, par], x_slots[part][bass.ds((n * 2 + (par - first_tile[part])) * TILE, TILE), :]
                              .rearrange("(s p) n -> p s n", p=P)).then_inc(s_xr[par], 16)

            def store_tile(n, par, part):
                done_apart(eng, s_yr[par], n + 1)
                eng.dma_start(y_slots[part][bass.ds((n * 2 + (par - first_tile[part])) * TILE, TILE), :]
                              .rearrange("(s p) n -> p s n", p=P), y_out[:, par]).then_inc(s_yst[par], 16)
            wait_scattered(0)
            for n in range(3):
                for par in range(2):
                    load_tile(n, par, 0)
            with eng.Fori(3, PART_TILES[0] // 2) as n:
                for par in range(2):
                    load_tile(n, par, 0)
                    store_tile(n - 3, par, 0)
            wait_scattered(1)
            for n in range(PART_TILES[0] // 2, PART_TILES[0] // 2 + 3):
                for par in range(2):
                    load_tile(n, par, 1)
                    store_tile(n - 3, par, 0)
            with eng.Fori(PART_TILES[0] // 2 + 3, NTILES // 2) as n:
                for par in range(2):
                    load_tile(n, par, 1)
                    store_tile(n - 3, par, 1)
            for n in range(NTILES // 2 - 3, NTILES // 2):
                for par in range(2):
                    store_tile(n, par, 1)

            with eng.Fori(0, NG // 2) as n:
                for par in range(2):
                    g = n * 2 + par
                    done_apart(eng, s_comb[par], n + 1)
                    eng.dma_start(out[bass.ds(g * GROUP, GROUP)].rearrange("b t n -> t b n"),
                                  h_all[0:T, bass.ds(g * GROUP, GROUP), :]).then_inc(s_out, 16)
            eng.wait_ge(s_out, 16 * NG)
            for h in range(2):
                eng.wait_ge(s_zero[h], 16 * clears[h])

        @block.gpsimd
        def _(pool):
            eng = pool
            nc.gpsimd.memset(epsc[:, 0], EPS)
            nc.gpsimd.memset(epsc[:, 1], -0.5)
            nc.gpsimd.memset(onesh[:], 1.0)
            nc.gpsimd.memset(ones64[:], 1.0).then_inc(s_const, 1)
            nc.gpsimd.memset(zeros[:], 0.0).then_inc(s_const, 2)
            eng.wait_ge(s_const, 3)

            def join_maxima(g):
                eng.wait_ge(s_mx, 4)
                nc.gpsimd.partition_all_reduce(mxall[:], mx[:], P, ABSMAX).then_inc(s_mxall, 1)

            def rstd1(g):
                done(eng, s_st1, g + 1)
                nc.gpsimd.tensor_tensor(ve1[0:T], mv1[0:T, :, 1], epsc[0:T, 0], ALU.add).then_inc(s_ve1, 1)
                done(eng, s_ve1, g + 1)
                nc.gpsimd.tensor_tensor(rs1[0:T], ve1[0:T], epsc[0:T, 1], ALU.pow).then_inc(s_rs1, 1)

            def rope_add(g):
                done(eng, s_s, g)
                done(eng, s_rp, g + 1)
                nc.gpsimd.tensor_tensor(q_t, rparts[:, 0], rparts[:, 1], ALU.add)
                nc.gpsimd.tensor_tensor(k_t, rparts[:, 2], rparts[:, 3], ALU.add).then_inc(s_rope, 1)

            def rstd2(g):
                done(eng, s_st2, g + 1)
                nc.gpsimd.tensor_tensor(ve2[0:T], mv2[0:T, :, 1], epsc[0:T, 0], ALU.add).then_inc(s_ve2, 1)
                done(eng, s_ve2, g + 1)
                nc.gpsimd.tensor_tensor(rs2[0:T], ve2[0:T], epsc[0:T, 1], ALU.pow).then_inc(s_rs2, 1)

            def add_b2(g):
                hg = h_all[0:T, bass.ds(g * GROUP, GROUP), :]
                nc.gpsimd.tensor_tensor(hg, hg, rowb[0:T, 3:4, :].to_broadcast([T, GROUP, D]), ALU.add).then_inc(s_hb2, 1)

            def scatter(n, part=0, buffers=range(2)):
                rows, b0 = ((rows_a, 0), (rows_b, PART_B[0]))[part]
                for par in buffers:
                    done_apart(eng, s_scat[par], n, 16 * TOP)
                    nc.gpsimd.tensor_copy(sidx[0:T, par], pos[0:T, bass.ds(n * 2 + par, 1), :].rearrange("p b k -> p (b k)")).then_inc(s_stage, 1)
                    nc.gpsimd.tensor_copy(srow[0:T, par].bitcast(F32), rows[0:T, bass.ds(n * 2 + (par - b0), 1), :].rearrange("p b n -> p (b n)").bitcast(F32)).then_inc(s_stage, 1)
                    done_apart(eng, s_stage, n * 2 + (par + 1), 2)
                    for k in range(TOP):
                        nc.gpsimd.indirect_dma_start(
                            x_slots[part], bass.IndirectOffsetOnAxis(ap=sidx[0:T, par, k:k + 1], axis=0),
                            srow[0:T, par], None).then_inc(s_scat[par], 16)

            def gather(n, par, part):
                done_apart(eng, s_gat[par], n, 16 * GROUP * TOP)
                done_apart(eng, s_comb[par], n)
                nc.gpsimd.tensor_copy(gidx[0:T, par], pos[0:T, bass.ds((n * 2 + par) * GROUP, GROUP), :]).then_inc(s_gidx, 1)
                done_apart(eng, s_gidx, n * 2 + par + 1)
                for b in range(GROUP):
                    for k in range(TOP):
                        nc.gpsimd.indirect_dma_start(
                            gat[0:T, par, b, k, :], None,
                            y_slots[part], bass.IndirectOffsetOnAxis(ap=gidx[0:T, par, b, k:k + 1], axis=0),
                        ).then_inc(s_gat[par], 16)

            def start_scatter():
                eng.wait_ge(s_routed, 1)
                eng.wait_ge(s_zero[0], 16 * PART_TILES[0] * TILE // CLEAR)
                eng.wait_ge(s_rows[0], 16)
                scatter(0)

            first_step = PART_GROUPS[0] + 1
            steps = range(first_step, first_step + PART_B[0] // 2 - 1)
            assert steps.stop <= NG + 1

            def scatter_even(i):
                scatter(i - steps.start + 1, 0, (0,))

            def scatter_odd(i):
                scatter(i - steps.start + 1, 0, (1,))

            pipeline(eng, [(rstd2, -1), (rstd1, 2), (scatter_even, 0, steps), (rope_add, 1), (join_maxima, 1, range(1)),
                           (scatter_odd, 0, steps)], start_scatter)
            eng.wait_ge(s_routed, 2)
            eng.wait_ge(s_zero[1], 16 * PART_TILES[1] * TILE // CLEAR)
            eng.wait_ge(s_rows[1], 16)
            with eng.Fori(PART_B[0] // 2, B // 2) as n:
                scatter(n, 1)

            eng.wait_ge(s_ysh, SJA)
            with eng.Fori(0, NG) as g:
                add_b2(g)

            def wait_stored(tiles):
                for par in range(2):
                    eng.wait_ge(s_yst[par], 16 * tiles // 2)

            wait_stored(PART_TILES[0])
            for par in range(2):
                gather(0, par, 0)
            full, odd = divmod(PART_GROUPS[0], 2)
            with eng.Fori(1, full) as n:
                for par in range(2):
                    gather(n, par, 0)
            if odd:
                gather(full, 0, 0)
            wait_stored(NTILES)
            if odd:
                gather(full, 1, 1)
            with eng.Fori(full + odd, NG // 2) as n:
                for par in range(2):
                    gather(n, par, 1)

        @block.tensor
        def _(pe):
            eng = pe

            def add_bias(bank, n):
                nc.tensor.matmul(bank[0:T, 0:GROUP * D], onesh[:, 0:T], bias[:, n:n + 1, :].to_broadcast([BPARTS, GROUP, D]),
                                 start=True, stop=False)

            def h_mm(g):
                done(eng, s_h, g)
                done(eng, s_x, g + 1, 16)
                if isinstance(g, int) and g == 0:
                    eng.wait_ge(s_first, 16 * N_FIRST)
                    eng.wait_ge(s_const, 3)
                    eng.wait_ge(s_bias, 1)
                add_bias(h_ps, 0)
                for b in range(GROUP):
                    for c in range(CTX):
                        last = nc.tensor.matmul(h_ps[0:T, b * D:(b + 1) * D], x_in[:, c, b * T:(b + 1) * T], wt[:, c, :],
                                                start=False, stop=(c == CTX - 1 and b == GROUP - 1))
                last.then_inc(s_h_mm, 1)

            def t1(g):
                done(eng, s_lg, g - 2)
                done(eng, s_lnt, g)
                done(eng, s_ln, g + 1)
                if isinstance(g, int) and g == 0:
                    eng.wait_ge(s_setup, 16 * N_SETUP)
                for b in range(GROUP):
                    last = nc.tensor.transpose(t1_ps[:, b * T:(b + 1) * T], ln[0:T, b, :], ident[0:T, 0:T])
                last.then_inc(s_t1, 1)

            def qk(g):
                done(eng, s_v, g)
                done(eng, s_h2, g - 1)
                done(eng, s_rp, g)
                done(eng, s_lnt, g + 1)
                for n, dst in enumerate((q_ps, qs_ps, k_ps, ks_ps)):
                    last = nc.tensor.matmul(dst[:, 0:GT], wmat[:, n, :], ln_t, start=True, stop=True)
                last.then_inc(s_qk, 1)

            def v_mm(g):
                done(eng, s_rp, g + 1)
                add_bias(v_ps, 1)
                for b in range(GROUP):
                    last = nc.tensor.matmul(v_ps[0:T, b * D:(b + 1) * D], ln_t[:, b * T:(b + 1) * T], wmat[:, 4, :],
                                            start=False, stop=(b == GROUP - 1))
                last.then_inc(s_v_mm, 1)

            def s_mm(g):
                done(eng, s_wei, g)
                done(eng, s_rope, g + 1)
                nc.tensor.matmul(s_ps[0:T, 0:GT], maskl[0:T, 0, 0:T],
                                 maskl[0:T, 1:2, 0:T].to_broadcast([T, GROUP, T]), start=True, stop=False)
                for b in range(GROUP):
                    c = slice(b * T, (b + 1) * T)
                    last = nc.tensor.matmul(s_ps[0:T, c], q_t[:, c], k_t[:, c], start=False, stop=(b == GROUP - 1))
                last.then_inc(s_s, 1)

            def pv(g):
                done(eng, s_xt, g - 1)
                done(eng, s_v, g + 1)
                done(eng, s_wei, g + 1)
                for b in range(GROUP):
                    c = slice(b * T, (b + 1) * T)
                    last = nc.tensor.matmul(pv_ps[:, c], v_tok[0:T, b, :], wei[0:T, c], start=True, stop=True)
                last.then_inc(s_pv, 1)

            def wp(g):
                done(eng, s_rp, upto(g + 2))
                done(eng, s_att, g + 1)
                add_bias(wp_ps, 2)
                for b in range(GROUP):
                    last = nc.tensor.matmul(wp_ps[0:T, b * D:(b + 1) * D], att_t[:, b * T:(b + 1) * T], wmat[:, 5, :],
                                            start=False, stop=(b == GROUP - 1))
                last.then_inc(s_wp, 1)

            t2_h = t2_ps.bitcast(F16)

            def t2(g):
                done(eng, s_att, upto(g + 2))
                done(eng, s_xlo, g + 1)
                for h in range(2):
                    for b in range(GROUP):
                        c = h * 512 + b * P
                        last = nc.tensor.transpose(t2_h[:, c:c + T], xsplit[0:T, b, h, :], identh[0:T, 0:T])
                last.then_inc(s_t2, 1)

            def lg(g):
                done(eng, s_lnt, upto(g + 3))
                done(eng, s_gs, 2)
                done(eng, s_xt, g + 1)
                for b in range(GROUP):
                    xh = xt_all[:, 0, bass.ds(g * GT + b * T, T)]
                    xl = xt_all[:, 1, bass.ds(g * GT + b * T, T)]
                    dst = lg_ps[0:T, b * E:(b + 1) * E]
                    nc.tensor.matmul(dst, xh, gsplit[:, 0], start=True, stop=False)
                    nc.tensor.matmul(dst, xh, gsplit[:, 1], start=False, stop=False)
                    last = nc.tensor.matmul(dst, xl, gsplit[:, 0], start=False, stop=True)
                last.then_inc(s_lg_mm, 1)

            def ranks(h):
                eng.wait_ge(s_chosen, h + 1)
                eng.wait_ge(s_xt, sum(PART_GROUPS[:h + 1]))
                if h == 1:
                    eng.wait_ge(s_h, NG)
                for n, dst in enumerate(rank_banks(h)):
                    last = nc.tensor.matmul(dst, tri[0:T, n, 0:T], chosen[0:T, 0:PART_B[h] * E], start=True, stop=True)
                last.then_inc(s_rank, 1)
                eng.wait_ge(s_rank_read, h + 1)

            pipeline(eng, [(t1, 1), (s_mm, 0), (qk, 1), (pv, 0), (h_mm, 3), (t2, -1), (v_mm, 1), (lg, -1), (wp, 0)], lambda: ranks(0))

            ranks(1)

            w8 = [w[:, :, :].bitcast(mybir.dt.uint8) for w in (whi, wlo)]

            def part(w, k, col, f):
                return w8[w][:, k, bass.ds(col * 2 + f * 2 * P, 2 * P)].bitcast(F16)

            def unit_up(u, par, x_hi, x_lo, n, col):
                done(eng, s_gelu, u - 1)
                for f in range(FC):
                    dst = pre_ps[:, par, f // 2, (f % 2) * TILE:(f % 2) * TILE + n]
                    hi, lo = part(0, 0, col, f), part(1, 0, col, f)
                    nc.tensor.matmul(dst, hi, x_hi, start=True, stop=False)
                    nc.tensor.matmul(dst, hi, x_lo, start=False, stop=False)
                    last = nc.tensor.matmul(dst, lo, x_hi, start=False, stop=True)
                    if f % 2:
                        last.then_inc(s_pre[f // 2], 1)

            def unit_down(u, par, m, dsts, col, first, final):
                done(eng, s_hlo, u + 1)
                for t in range(2):
                    for f in range(FC):
                        h = hhi[:, par, f, t * m:(t + 1) * m]
                        l = hlo[:, par, f, t * m:(t + 1) * m]
                        hi, lo = part(0, 1, col, f), part(1, 1, col, f)
                        nc.tensor.matmul(dsts[t], h, hi, start=first and f == 0, stop=False)
                        nc.tensor.matmul(dsts[t], h, lo, start=False, stop=False)
                        last = nc.tensor.matmul(dsts[t], l, hi, start=False, stop=final and f == FC - 1)
                last.then_inc(s_y_mm, 1)

            xp_h = [xp_ps[:, p, :].bitcast(F16) for p in range(2)]

            def transpose_tile(n, par):
                done(eng, s_xrt[par], n)
                done(eng, s_xr[par], n + 1, 16)
                for h in range(2):
                    for s in range(SUB):
                        c = h * TILE + s * P
                        last = nc.tensor.transpose(xp_h[par][:, c:c + P], xr_in[:, par, s, h * D:(h + 1) * D], identh[:])
                last.then_inc(s_xp[par], 1)

            def up_step(u, kind, n, par, expert):
                if kind == "shared":
                    cols = bass.ds(n * 2 * T, 2 * T)
                    unit_up(u, par, xt_all[:, 0, cols], xt_all[:, 1, cols], 2 * T, (E + par) * F)
                if kind == "routed":
                    done(eng, s_xrt[par], n + 1)
                    unit_up(u, par, xr_t[:, par, 0], xr_t[:, par, 1], TILE, expert * F)

            def addresses(kind, k, expert):
                if kind == "routed":
                    for f in range(FC):
                        for w in range(2):
                            pe.lower_ap(part(w, k, expert * F, f))

            def down_step(u, kind, n, par, expert):
                if kind == "shared":
                    if par == 0:
                        done(eng, s_ysh, n)
                        if isinstance(n, int) and n == SJA:
                            for p in range(2):
                                eng.wait_ge(s_yr[p], NTILES // 2)
                    unit_down(u, par, T, [y_ps[0:T, t, 0:D] for t in range(2)], (E + par) * F, par == 0, par == 1)
                if kind == "routed":
                    if isinstance(n, int) and n == 0:
                        eng.wait_ge(s_ysh, SJA)
                    done(eng, s_yr[par], n)
                    unit_down(u, par, P, [y_ps[:, par, s * D:(s + 1) * D] for s in range(SUB)], expert * F, True, True)

            def pe_step(p, pair, i, c):
                (kind0, n0), (kind1, n1), (kind2, n2) = pair(0), pair(1), pair(2)
                experts = [0] * 4
                if kind2 == "routed" and isinstance(n2, int) and n2 == 0:
                    eng.wait_ge(s_tiles, 2)
                if "routed" in (kind0, kind1, kind2):
                    n = n0 if kind0 == "routed" else n1 - 1 if kind1 == "routed" else n2 - 2
                    experts = experts_of(mybir.EngineType.PE, n, 0, 4)
                for par in range(2):
                    addresses(kind0, 1, experts[par])
                    down_step(p * 2 + par, kind0, n0, par, experts[par])
                    if kind2 == "routed":
                        transpose_tile(n2, par)
                    if par == 0:
                        addresses(kind1, 0, experts[2])
                        up_step(p * 2 + 3, kind1, n1, 1, experts[2])
                    else:
                        addresses(kind2, 0, experts[3])
                        up_step(p * 2 + 4, kind2, n2, 0, experts[3])

            eng.wait_ge(s_wlo, WGROUPS)
            eng.wait_ge(s_xt, NG)
            run_units(eng, pe_step)

        @block.scalar
        def _(act):
            eng = act

            def load_table(table):
                eng.add_instruction(mybir.InstLoadActFuncSet(
                    name=nc.get_next_instruction_name(), engine=mybir.EngineType.Activation, act_func_set_id=table))

            def softplus_abs(g):
                done(eng, s_s, g + 1)
                nc.scalar.activation(sp[0:T], s_ps[0:T, 0:GT], ACT.Abs).then_inc(s_abs, 1)

            def softplus_log(g):
                done(eng, s_abs, g + 1)
                nc.scalar.activation(sp[0:T], sp[0:T], ACT.Exp, scale=-1.0).then_inc(s_exp, 1)
                done(eng, s_exp, g + 1)
                nc.scalar.activation(sp[0:T], sp[0:T], ACT.Ln, bias=1.0).then_inc(s_lnp, 1)

            def ln_t_out(g):
                done(eng, s_v_mm, g)
                done(eng, s_t1, g + 1)
                nc.scalar.activation(ln_t, t1_ps[:, 0:GT], ACT.Copy).then_inc(s_lnt, 1)

            def att_out(g):
                done(eng, s_wp, g)
                done(eng, s_pv, g + 1)
                nc.scalar.activation(att_t, pv_ps[:, 0:GT], ACT.Copy).then_inc(s_att, 1)

            def h_out(g):
                done_apart(eng, s_h_mm, g + 1)
                nc.scalar.activation(h_all[0:T, bass.ds(g * GROUP, GROUP), :],
                                     h_ps[0:T, 0:GROUP * D].rearrange("p (b n) -> p b n", n=D), ACT.Copy).then_inc(s_h, 1)

            def v_out(g):
                done(eng, s_pv, g)
                done(eng, s_v_mm, g + 1)
                nc.scalar.activation(v_tok[0:T], v_ps[0:T, 0:GROUP * D].rearrange("p (b n) -> p b n", n=D), ACT.Copy).then_inc(s_v, 1)

            def x_t_out(g):
                done_apart(eng, s_t2, g + 1)
                nc.scalar.activation(
                    xt_all[:, :, bass.ds(g * GT, GT)].rearrange("p h (b t) -> p h b t", b=GROUP),
                    t2_ps.bitcast(F16).rearrange("p (h b t) -> p h b t", h=2, b=GROUP)[:, :, :, 0:T], ACT.Copy).then_inc(s_xt, 1)

            def logits_out(g):
                done_apart(eng, s_lg_mm, g + 1)
                nc.scalar.activation(logits[0:T, bass.ds(g * GROUP, GROUP), :],
                                     lg_ps[0:T, 0:GROUP * E].rearrange("p (b e) -> p b e", e=E), ACT.Copy,
                                     scale=down[0:T, 3:4]).then_inc(s_lg, 1)

            def w_high(g):
                if isinstance(g, int) and g == 0:
                    eng.wait_ge(s_gs, 2)
                for n, scale in ((0, up[:, 0:1]), (1, up[:, 2:3])):
                    c = split_columns(g)
                    last = nc.scalar.activation(whi[:, n, c], w32[:, n, c], ACT.Copy, scale=scale)
                last.then_inc(s_whi, 1)

            def router_exp(h):
                eng.wait_ge(s_centred, h + 1)
                b, n = sum(PART_B[:h]), PART_B[h]
                nc.scalar.activation(ra_all[0:T, 0:n * E].rearrange("p (b e) -> p b e", e=E), logits[0:T, b:b + n], ACT.Exp).then_inc(s_rexp, 1)

            load_table(EXP_LN_TABLE)
            pipeline(eng, [(ln_t_out, 1), (softplus_abs, 0), (softplus_log, 0), (w_high, 0, range(1, WGROUPS)), (att_out, 0),
                           (h_out, 3), (x_t_out, -1), (v_out, 1), (logits_out, -1), (w_high, 0, range(1))],
                     lambda: router_exp(0))

            router_exp(1)

            def gelu(u, par, n, col):
                done_apart(eng, s_hlo, u - 1)
                for f in range(FC):
                    if f % 2 == 0:
                        done_apart(eng, s_pre[f // 2], u + 1)
                    last = nc.scalar.activation(gel[:, par, f * TILE:f * TILE + n],
                                                pre_ps[:, par, f // 2, (f % 2) * TILE:(f % 2) * TILE + n], ACT.Gelu,
                                                bias=b1[:, bass.ds(col + f, 1)], scale=down[:, 0:1])
                last.then_inc(s_gelu, 1)

            def last_high(u, par):
                done(eng, s_y_mm, u - 1)
                done(eng, s_gelu, u + 1)
                nc.scalar.activation(hhi[:, par, FC - 1, 0:2 * T], gel4[:, par, FC - 1, 0:2 * T], ACT.Copy,
                                     scale=up[:, 1:2]).then_inc(s_last_high, 1)

            def xr_out(u, n, par):
                done(eng, s_pre[1], u - 1)
                done(eng, s_xp[par], n + 1)
                nc.scalar.activation(xr_t[:, par].rearrange("p h n -> p (h n)"),
                                     xp_ps[:, par, :].bitcast(F16)[:, 0:2 * TILE], ACT.Copy).then_inc(s_xrt[par], 1)

            def act_step(p, pair, i, c):
                (kind0, _), (kind1, n1), (kind2, n2) = pair(0), pair(1), pair(2)
                experts = [0] * 2
                if kind2 == "routed" and isinstance(n2, int) and n2 == 0:
                    eng.wait_ge(s_tiles, 2)
                if "routed" in (kind1, kind2):
                    experts = experts_of(mybir.EngineType.Activation, n1 - 1 if kind1 == "routed" else n2 - 2, 2, 4)
                for par in range(2):
                    if kind2 == "routed":
                        xr_out(p * 2 + 4 + par, n2, par)
                    kind, u = (kind1, p * 2 + 3) if par == 0 else (kind2, p * 2 + 4)
                    if kind == "shared":
                        gelu(u, 1 - par, 2 * T, (E + 1 - par) * FC)
                        last_high(u, 1 - par)
                    if kind == "routed":
                        gelu(u, 1 - par, TILE, experts[par] * FC)

            load_table(GELU_TABLE)
            eng.wait_ge(s_wlo, WGROUPS)
            run_units(eng, act_step)

        @block.vector
        def _(dve):
            eng = dve
            chain = [0]

            def link(ins):
                chain[0] += 1
                ins.then_inc(s_scale, 1)
                dve.wait_ge(s_scale, chain[0])

            eng.wait_ge(s_first, 16 * N_FIRST)
            n_b = [0]

            def link_b(ins):
                n_b[0] += 1
                ins.then_inc(s_bias_chain, 1)
                dve.wait_ge(s_bias_chain, n_b[0])

            rest = bias_parts[:, 3]
            link_b(nc.vector.tensor_copy(rest, rowb[0:BPARTS, 0:3, :]))
            for k in range(BPARTS):
                link_b(nc.vector.tensor_copy(part16[:], rest))
                link_b(nc.vector.tensor_copy(bias_parts[:, k], part16[:]))
                link_b(nc.vector.tensor_tensor(rest, rest, bias_parts[:, k], ALU.subtract))
            link_b(nc.vector.tensor_scalar(rest, bias_parts[:, 0], ident[0:BPARTS, 0:1], None, ALU.mult))
            link_b(nc.vector.scalar_tensor_tensor(rest, bias_parts[:, 1], ident[0:BPARTS, 1:2], rest, ALU.mult, ALU.add))
            link_b(nc.vector.scalar_tensor_tensor(rest, bias_parts[:, 2], ident[0:BPARTS, 2:3], rest, ALU.mult, ALU.add))
            nc.vector.tensor_copy(bias[:], rest).then_inc(s_bias, 1)

            def maximum(n, src):
                nc.vector.tensor_reduce(mx[:, n:n + 1], src, X, ALU.max, apply_absolute_value=True).then_inc(s_mx, 1)

            def max_w1(g):
                eng.wait_ge(s_w32[0], 16 * 2)
                maximum(0, w32[:, 0, :])

            def max_w2(g):
                eng.wait_ge(s_setup, 16 * N_SETUP)
                maximum(1, b1[:])
                maximum(3, gatew[:])
                eng.wait_ge(s_w32[1], 16 * 2)
                maximum(2, w32[:, 1, :])

            def scales(g):
                eng.wait_ge(s_mxall, 1)
                link(nc.vector.scalar_tensor_tensor(mxall[:, 1:2], mxall[:, 0:1], float(D), mxall[:, 1:2], ALU.mult, ALU.add))
                link(nc.vector.tensor_scalar(mxall[:], mxall[:], LEAST, None, ALU.max))
                link(nc.vector.tensor_scalar(pw[:].bitcast(I32), mxall[:].bitcast(I32), TOPBITS, None, ALU.bitwise_and))
                link(nc.vector.reciprocal(up[:], pw[:]))
                link(nc.vector.tensor_scalar(up[:], up[:], LIFT, None, ALU.mult))
                link(nc.vector.tensor_scalar(down[:], pw[:], 1.0 / LIFT, None, ALU.mult))
                link(nc.vector.tensor_tensor(yscale[:], down[:, 1:2], down[:, 2:3], ALU.mult))
                link(nc.vector.tensor_tensor(rowb[:, 3, :], rowb[:, 3, :], rowb[:, 4, :], ALU.add))
                nc.vector.tensor_scalar(gsplit[:, 0], gatew[:], up[:, 3:4], None, ALU.mult).then_inc(s_gs, 1)
                eng.wait_ge(s_gs, 1)
                nc.vector.scalar_tensor_tensor(gsplit[:, 1], gatew[:], up[:, 3:4], gsplit[:, 0], ALU.mult, ALU.subtract).then_inc(s_gs, 1)

            def rows(g):
                return h_all[0:T, bass.ds(g * GROUP, GROUP), :]

            def stats(g, st, s_src, s_a):
                done_apart(eng, s_src, g + 1)
                for b in range(GROUP):
                    last = nc.vector.bn_stats(st[0:T, b, :], rows(g)[:, b, :])
                last.then_inc(s_a, 1)

            def moments(g, st, mv, s_a, s_before, s_done):
                done_apart(eng, s_before, g)
                done_apart(eng, s_a, g + 1)
                for b in range(GROUP):
                    last = nc.vector.bn_aggr(mv[0:T, b, :], st[0:T, b, :])
                last.then_inc(s_done, 1)

            def stats1(g):
                done_apart(eng, s_st1, g)
                stats(g, st1, s_h, s_st1a)

            def stats2(g):
                done_apart(eng, s_st2, g)
                stats(g, st2, s_h2, s_st2a)

            def moments1(g):
                moments(g, st1, mv1, s_st1a, s_ln, s_st1)

            def moments2(g):
                moments(g, st2, mv2, s_st2a, s_xn, s_st2)

            def ln_out(g):
                done(eng, s_t1, g)
                done(eng, s_rs1, g + 1)
                for b in range(GROUP):
                    last = nc.vector.tensor_scalar(ln[0:T, b, :], h_all[0:T, bass.ds(g * GROUP + b, 1), :].rearrange("p b n -> p (b n)"),
                                                   mv1[0:T, b, 0:1], rs1[0:T, b:b + 1], ALU.subtract, ALU.mult)
                last.then_inc(s_ln, 1)

            def rope_parts(g):
                done(eng, s_rope, g)
                done(eng, s_qk, g + 1)
                for n, src in enumerate((q_ps, qs_ps, k_ps, ks_ps)):
                    last = nc.vector.scalar_tensor_tensor(
                        rparts[:, n].rearrange("p (b t) -> p b t", t=T), src[:, 0:GT].rearrange("p (b t) -> p b t", t=T),
                        colb[:, n:n + 1], rope[:, n:n + 1, :].to_broadcast([P, GROUP, T]), ALU.add, ALU.mult)
                last.then_inc(s_rp, 1)

            def weights(g):
                done(eng, s_pv, g)
                done(eng, s_lnp, g + 1)
                nc.vector.scalar_tensor_tensor(wei[0:T], s_ps[0:T, 0:GT], 0.0, sp[0:T], ALU.max, ALU.add).then_inc(s_wei, 1)

            def h2_out(g):
                done(eng, s_ln, g + 1)
                done(eng, s_wp, g + 1)
                nc.vector.tensor_tensor(rows(g), wp_ps[0:T, 0:GROUP * D].rearrange("p (b n) -> p b n", n=D), rows(g),
                                        ALU.add).then_inc(s_h2, 1)

            def x_out(g):
                done(eng, s_xlo, g)
                done(eng, s_rs2, g + 1)
                for b in range(GROUP):
                    last = nc.vector.tensor_scalar(xn[0:T, b, :], h_all[0:T, bass.ds(g * GROUP + b, 1), :].rearrange("p b n -> p (b n)"),
                                                   mv2[0:T, b, 0:1], rs2[0:T, b:b + 1], ALU.subtract, ALU.mult)
                last.then_inc(s_xn, 1)
                done(eng, s_t2, g)
                done(eng, s_xtok, g, 16)
                done(eng, s_xn, g + 1)
                nc.vector.tensor_copy(xsplit[0:T, :, 0, :], xn[0:T]).then_inc(s_xhi, 1)
                done(eng, s_xhi, g + 1)
                nc.vector.tensor_tensor(xsplit[0:T, :, 1, :], xn[0:T], xsplit[0:T, :, 0, :], ALU.subtract).then_inc(s_xlo, 1)

            def w_low(g):
                done(eng, s_whi, g + 1)
                for n, scale in ((0, up[:, 0:1]), (1, up[:, 2:3])):
                    c = split_columns(g)
                    last = nc.vector.scalar_tensor_tensor(wlo[:, n, c], w32[:, n, c], scale, whi[:, n, c], ALU.mult, ALU.subtract)
                last.then_inc(s_wlo, 1)

            n_r = [0]

            def link_r(ins):
                n_r[0] += 1
                ins.then_inc(s_r, 1)
                dve.wait_ge(s_r, n_r[0])

            def routing(h):
                nb, b0 = PART_B[h], sum(PART_B[:h])

                def over_e(v):
                    return v.rearrange("p (b e) -> p b e", e=1).to_broadcast([T, nb, E])

                def over_b(v):
                    return v.rearrange("p (b e) -> p b e", b=1).to_broadcast([T, nb, E])

                L = logits[0:T, b0:b0 + nb]
                A, C = (v[0:T, 0:nb * E].rearrange("p (b e) -> p b e", e=E) for v in (ra_all, rc_all))
                run = run_all[0:T, 0:nb * E].rearrange("p (e b) -> p e b", e=E)
                oh = oh_all[0:T, :, 0:nb * E].rearrange("p k (b e) -> p k b e", e=E)
                gate_values = gatev[0:T, :, b0:b0 + nb]
                v = [rvec[0:T, n, 0:nb] for n in range(4)]
                eng.wait_ge(s_lg, sum(PART_GROUPS[:h + 1]))
                eng.wait_ge(s_wlo, WGROUPS)
                link_r(nc.vector.tensor_tensor(L, L, over_b(gateb[0:T]), ALU.add))
                link_r(nc.vector.tensor_reduce(v[0], L, X, ALU.max))
                nc.vector.tensor_tensor(L, L, over_e(v[0]), ALU.subtract).then_inc(s_centred, 1)
                eng.wait_ge(s_rexp, h + 1)
                link_r(nc.vector.tensor_reduce(v[1], A, X, ALU.add))
                link_r(nc.vector.reciprocal(v[2], v[1]))
                link_r(nc.vector.tensor_tensor(A, A, over_e(v[2]), ALU.mult))
                src = A
                for k in range(TOP):
                    link_r(nc.vector.tensor_reduce(gate_values[:, k], src, X, ALU.max))
                    link_r(nc.vector.tensor_tensor(C, src, over_e(gate_values[:, k]), ALU.is_equal))
                    link_r(nc.vector.tensor_tensor(C, C, over_b(prefer_low[0:T]), ALU.mult))
                    link_r(nc.vector.tensor_reduce(v[3], C, X, ALU.max))
                    link_r(nc.vector.tensor_tensor(oh[:, k], over_b(prefer_low[0:T]), over_e(v[3]), ALU.is_equal))
                    if k == 0:
                        link_r(nc.vector.scalar_tensor_tensor(C, oh[:, 0], -2.0, A, ALU.mult, ALU.add))
                        src = C
                nc.vector.tensor_tensor(chosen[0:T, 0:nb * E].rearrange("p (b e) -> p b e", e=E), oh[:, 0], oh[:, 1], ALU.add).then_inc(s_chosen, 1)
                eng.wait_ge(s_rank, h + 1)
                rank, total = (v.rearrange("p (b e) -> p b e", e=E) for v in rank_banks(h))
                for e in range(E):
                    last = nc.vector.tensor_tensor_scan(run[:, e, :], ones64[0:T, 0:nb], total[:, :, e], 0.0, ALU.mult, ALU.add)
                link_r(last)
                link_r(nc.vector.tensor_tensor(A, run.rearrange("p e b -> p b e"), total, ALU.subtract))
                nc.vector.tensor_tensor(A, A, rank, ALU.add).then_inc(s_rank_read, 1)
                eng.wait_ge(s_rank_read, h + 1)
                full = cmp[0:T, 0:E * MAXT].rearrange("p (e n) -> p e n", e=E)
                link_r(nc.vector.tensor_copy(te[0:T, 0], run[:, :, nb - 1]))
                link_r(nc.vector.tensor_tensor(full, te[0:T, 0].rearrange("p (e n) -> p e n", n=1).to_broadcast([T, E, MAXT]),
                                               tile_steps[0:T].rearrange("p (e n) -> p e n", e=1).to_broadcast([T, E, MAXT]), ALU.is_gt))
                link_r(nc.vector.tensor_reduce(te[0:T, 1], full, X, ALU.add))
                link_r(nc.vector.tensor_tensor_scan(te[0:T, 2], ones64[0:T, 0:E], te[0:T, 1], 0.0, ALU.mult, ALU.add))
                link_r(nc.vector.tensor_tensor(te[0:T, 3], te[0:T, 2], te[0:T, 1], ALU.subtract))
                link_r(nc.vector.tensor_scalar(te[0:T, 3], te[0:T, 3], float(TILE), None, ALU.mult))
                link_r(nc.vector.tensor_tensor(A, A, over_b(te[0:T, 3]), ALU.add))
                for k in range(TOP):
                    link_r(nc.vector.tensor_tensor(C, oh[:, k], A, ALU.mult))
                    link_r(nc.vector.tensor_reduce(posf[0:T, 0:nb, k], C, X, ALU.add))
                nc.vector.tensor_copy(pos[0:T, b0:b0 + nb], posf[0:T, 0:nb]).then_inc(s_routed, 1)

            def tile_table(h):
                tiles, t0 = PART_TILES[h], sum(PART_TILES[:h])
                passed = cmp[0:1, 0:tiles * (E - 1)].rearrange("p (n e) -> p n e", e=E - 1)
                link_r(nc.vector.tensor_tensor(passed, tile_ids[0:1, 0:tiles].rearrange("p (n e) -> p n e", e=1).to_broadcast([1, tiles, E - 1]),
                                               te[0:1, 2, 0:E - 1].rearrange("p (n e) -> p n e", n=1).to_broadcast([1, tiles, E - 1]), ALU.is_ge))
                link_r(nc.vector.tensor_reduce(tile_exf[:, 0:tiles], passed, X, ALU.add))
                by_pair = tile_exf[:, 0:tiles].rearrange("p (n k) -> p n k", k=2)
                for lo, hi, row, k in ((0, 2, 2, 0), (2, 3, 1, 1), (3, 4, 0, 0)):
                    row += t0 // 2
                    last = nc.vector.tensor_copy(tile_ex[:, row:row + tiles // 2, lo:hi], by_pair[:, :, k:k + hi - lo])
                    if lo < 3:
                        link_r(last)
                last.then_inc(s_tiles, 1)

            def route_first():
                routing(0)
                tile_table(0)

            link_r(nc.vector.memset(tile_ex[:], 0))
            pipeline(eng, [(h2_out, -1), (stats1, 2), (stats2, -1), (moments1, 2), (moments2, -1),
                           (weights, 0), (x_out, -1), (rope_parts, 1), (ln_out, 2), (max_w1, 2, range(1)), (max_w2, 1, range(1)), (scales, 0, range(1)),
                           (w_low, 0, range(WGROUPS))], route_first)
            routing(1)

            def hidden(par, n, chunks=FC):
                return (v[:, par, 0:chunks, 0:n] for v in (gel4, hhi, hlo))

            def split_high(u, par, n, shared):
                g, high, _ = hidden(par, n, FC - 1 if shared else FC)
                done(eng, s_y_mm, u - 1)
                done(eng, s_gelu, u + 1)
                nc.vector.tensor_scalar(high, g, up[:, 1:2], None, ALU.mult).then_inc(s_hhi, 1)

            def split_low(u, par, n, shared, j):
                g, high, low = hidden(par, n)
                done(eng, s_hhi, u + 1)
                if shared:
                    done(eng, s_last_high, j * 2 + par + 1)
                nc.vector.scalar_tensor_tensor(low, g, up[:, 1:2], high, ALU.mult, ALU.subtract).then_inc(s_hlo, 1)

            def add_shared(u, j):
                if isinstance(j, int) and j == SJA:
                    eng.wait_ge(s_hb2, NG)
                done(eng, s_y_mm, u + 1)
                hj = h_all[0:T, bass.ds(j * 2, 2), :]
                nc.vector.scalar_tensor_tensor(hj, y_ps[0:T, :, 0:D], yscale[0:T], hj, ALU.mult, ALU.add).then_inc(s_ysh, 1)

            def tile_output(u, n, par, e):
                done(eng, s_yst[par], n, 16)
                done(eng, s_y_mm, u + 1)
                nc.vector.scalar_tensor_tensor(
                    y_out[:, par], y_ps[:, par, 0:SUB * D].rearrange("p (s n) -> p s n", n=D), yscale[:],
                    b2[:, bass.ds(e, 1), :].to_broadcast([P, SUB, D]), ALU.mult, ALU.add).then_inc(s_yr[par], 1)

            def combine(i, g0, part):
                n, par = i + g0 // 2, g0 % 2
                g = n * 2 + par
                k = part // 2
                if part == 0:
                    done(eng, s_gat[par], n + 1, 16 * GROUP * TOP)
                    done(eng, s_ysh, (g + 1) * 2)
                if k == 1:
                    done(eng, s_quarter, g * 3 + part - 1)
                for b in range(GROUP // 2 * (part % 2), GROUP // 2 * (part % 2 + 1)):
                    row = h_all[0:T, bass.ds(g * GROUP + b, 1), :].rearrange("p b n -> p (b n)")
                    last = nc.vector.scalar_tensor_tensor(
                        row, gat[0:T, par, b, k, :], gatev[0:T, k, bass.ds(g * GROUP + b, 1)], row, ALU.mult, ALU.add)
                last.then_inc(s_quarter if part < 3 else s_comb[par], 1)

            starts_b = SJA + NTILES // 2
            EARLY = 2 * TURN_GROUPS
            assert EARLY < PART_GROUPS[0] and 2 * PART_GROUPS[0] <= SJA
            starts_early = SJA + 2 + (NTILES // 2 - 4 - 4 * EARLY) // 4 * 4
            assert starts_early > SJA + PART_TILES[0] // 2

            def dve_step(p, pair, i, c):
                (kind0, n0), (kind1, n1) = pair(0), pair(1)
                if kind0 == "routed":
                    experts = experts_of(mybir.EngineType.DVE, n0, 0, 2)
                for par in range(2):
                    shared = kind1 == "shared"
                    if kind1 is not None:
                        split_high(p * 2 + 2 + par, par, 2 * T if shared else TILE, shared)
                    if kind0 == "shared" and par == 1:
                        add_shared(p * 2 + 1, n0)
                    if kind0 == "routed":
                        tile_output(p * 2 + par, n0, par, experts[par])
                    early, late = c - starts_early, c - starts_b
                    if par == 1 and 0 <= early < 4 * EARLY:
                        combine(i, early // 4, early % 4)
                    if late >= 0:
                        combine(i, EARLY + late // 2, late % 2 * 2 + par)
                    if kind1 is not None:
                        split_low(p * 2 + 2 + par, par, 2 * T if shared else TILE, shared, n1)
                if isinstance(p, int) and p == 0:
                    tile_table(1)

            run_units(eng, dve_step, unroll=4, cut=starts_early)
            for quarter in range(4 * EARLY + 2 * (SJ - SJA), 4 * NG):
                combine(0, quarter // 4, quarter % 4)


def kernel(**inputs):
    import numpy as np
    import concourse.bacc as bacc
    from concourse.bass_utils import run_bass_kernel_spmd
    import ml_dtypes

    def arr(name):
        return np.asarray(inputs[name])

    def cols(v):
        return v.reshape(-1, 1)

    def on_all(v):
        return np.broadcast_to(v, (P,) + v.shape)

    swap = np.arange(D).reshape(-1, 2)[:, ::-1].reshape(-1)
    where = np.arange(T - 1, -1, -1, dtype=np.float32)
    angle = (where[None, :] * np.arange(D // 2, dtype=np.float32)[:, None]).astype(np.float64)
    cos = np.repeat(np.cos(angle), 2, axis=0)
    sin = np.repeat(np.sin(angle), 2, axis=0) * np.tile([-1.0, 1.0], D // 2)[:, None]
    q_scale = float(D) ** -0.5
    rope = np.stack([cos * q_scale, sin * q_scale, cos, sin], axis=1).astype(np.float32)
    eye = np.eye(P)
    masked = np.where(np.arange(P)[None, :] < np.arange(P)[:, None], -1e30, 0.0)
    earlier = (np.arange(P)[:, None] < np.arange(P)[None, :]).astype(np.float32)
    counts = np.concatenate([np.arange(MAXT) * TILE, np.arange(PTILES), E - np.arange(E)]).astype(np.float32)

    wq, wk, bq, bk = arr("L0_attn_Wq"), arr("L0_attn_Wk"), arr("L0_attn_bq"), arr("L0_attn_bk")
    arrays = {
        "x": arr("x").reshape(B * T, CTX, D).transpose(2, 1, 0),
        "wt": arr("L0_tok_weight").reshape(D, CTX, D).transpose(2, 1, 0),
        "wmat": np.stack([wq, wq[:, swap], wk, wk[:, swap], arr("L0_attn_Wv"), arr("L0_attn_Wp")], axis=1),
        "rope": rope,
        "colb": np.concatenate([cols(bq), cols(bq[swap]), cols(bk), cols(bk[swap])], axis=1),
        "rowb": on_all(np.stack([arr("L0_tok_bias"), arr("L0_attn_bv"), arr("L0_attn_bp"),
                                 arr("L0_ffn_sb2")[0], arr("L0_ffn_sb2")[1]])),
        "gateb": on_all(arr("L0_ffn_gate_b")),
        "gatew": arr("L0_ffn_gate_w").T,
        "rb1": arr("L0_ffn_rb1").reshape(E * FC, P).T,
        "sb1": arr("L0_ffn_sb1").reshape(NS * FC, P).T,
        "rb2": on_all(arr("L0_ffn_rb2")),
        "rw1": arr("L0_ffn_rw1").transpose(2, 0, 1).reshape(D, E * F),
        "sw1": arr("L0_ffn_sw1").transpose(2, 0, 1).reshape(D, NS * F),
        "rw2": arr("L0_ffn_rw2").reshape(E, D, FC, P).transpose(3, 0, 2, 1).reshape(P, E * F),
        "sw2": arr("L0_ffn_sw2").reshape(NS, D, FC, P).transpose(3, 0, 2, 1).reshape(P, NS * F),
        "ident": eye.astype(np.float32),
        "identh": eye.astype(np.float16),
        "maskl": np.stack([eye, masked], axis=1).astype(ml_dtypes.bfloat16),
        "tri": np.stack([earlier, np.ones((P, P), np.float32)], axis=1).astype(ml_dtypes.bfloat16),
        "counts": on_all(counts),
    }
    arrays = {k: np.ascontiguousarray(v) for k, v in arrays.items()}
    nc = bacc.Bacc("TRN2", target_bir_lowering=False, num_devices=1)
    d = {k: nc.dram_tensor(f"in_{k}", v.shape, mybir.dt.from_np(v.dtype), kind="ExternalInput").ap() for k, v in arrays.items()}
    out = nc.dram_tensor("out", [B, T, D], F32, kind="ExternalOutput").ap()
    build(nc, d, out)
    r = run_bass_kernel_spmd(nc, [{f"in_{k}": v for k, v in arrays.items()}], core_ids=[0])
    return r.results[0]["out"]
```
